# Optimizing a Trainium2 kernel written in Bass

```python
import numpy as np
import jax
import jax.numpy as jnp

def _softmax(x, axis=-1):
    return jax.nn.softmax(x, axis=axis)

def _gelu(x):
    return jax.nn.gelu(x, approximate=True)

def _silu(x):
    return jax.nn.silu(x)

def _sigmoid(x):
    return jax.nn.sigmoid(x)

def _layernorm(x, axis=-1, eps=1e-05):
    m = jnp.mean(x, axis=axis, keepdims=True)
    v = jnp.var(x, axis=axis, keepdims=True)
    return (x - m) / jnp.sqrt(v + eps)

def _scatter_add(tgt, idx, src, axis=0):
    return tgt.at[idx].add(src)

def _segment_sum(src, seg, n):
    return jax.ops.segment_sum(src, seg, n)
kernel_name = 'mk_xattn_ffn_d1_seqx_r4_d671fd'

def setup_inputs(seed: int=0):
    np.random.seed(seed)
    _w = jnp.asarray

    def _rec_inputs():
        import jax
        import jax.numpy as jnp
        _rk = jax.random.key(seed)
        x = -0.000125 + 0.9999 * jax.random.normal(jax.random.fold_in(_rk, 1), (64, 128, 512), jnp.float32)
        _lenS = 128 - jax.random.randint(jax.random.fold_in(_rk, 7), (64,), 0, max(1, 128 // 4) + 1, jnp.int32)
        _lenS2 = 128 - jax.random.randint(jax.random.fold_in(_rk, 8), (64,), 0, max(1, 128 // 4) + 1, jnp.int32)
        _ctx_2048P = jax.random.normal(jax.random.fold_in(_rk, 11), (64, 16, 512), jnp.float32)
        _ctx_2048c = jax.random.dirichlet(jax.random.fold_in(_rk, 511), 0.3 * jnp.ones((16,), jnp.float32), (64, 128))
        _ctx_2048t = jnp.einsum('bsk,bkd->bsd', _ctx_2048c, _ctx_2048P)
        _ctx_2048t = _ctx_2048t * jax.lax.rsqrt(jnp.mean(jnp.square(_ctx_2048t)) + 1e-12) * 0.953939
        ctx_2048 = -0.000514642 + 1.00011 * (_ctx_2048t + 0.3 * jax.random.normal(jax.random.fold_in(_rk, 611), (64, 128, 512), jnp.float32))
        _validS = jnp.arange(128)[None, :] < _lenS[:, None]
        _validS2 = jnp.arange(128)[None, :] < _lenS2[:, None]
        _causal = jnp.tril(jnp.ones((128, 128), dtype=bool))
        mask_BxS2_bk0 = jnp.logical_not(jnp.broadcast_to(_validS2[:, :], (64, 128)))
        return (x, ctx_2048, mask_BxS2_bk0)
    x, ctx_2048, mask_BxS2_bk0 = _rec_inputs()

    def _L0_xattn_setup():
        import jax, jax.numpy as jnp
        import numpy as np
        key = jax.random.key(seed)
        k1, k2, k3 = jax.random.split(key, 3)
        B, S, D, M = (8, 512, 512, 128)
        hidden_states = jax.random.normal(k1, (B, S, D), dtype=jnp.float32)
        memory_tokens = jax.random.normal(k2, (B, M, D), dtype=jnp.float32)
        memory_mask = jax.random.randint(k3, (B, M), 0, 2).astype(jnp.bool_)
        return {'hidden_states': hidden_states, 'memory_tokens': memory_tokens, 'memory_mask': memory_mask}
    _L0_xattn_all = _L0_xattn_setup()
    _L0_xattn_in = {k: v for k, v in _L0_xattn_all.items() if k in ()}
    del _L0_xattn_all

    def _L0_ffn_setup():
        import jax, jax.numpy as jnp
        import numpy as np
        B, S, H = (4, 512, 512)
        E = 8
        F = H // E
        TOPK = 2
        LORA_R = 16
        LORA_SCALE = 1.0
        key = jax.random.key(seed)
        ks = jax.random.split(key, 7)
        x = jax.random.normal(ks[0], (B, S, H), dtype=jnp.float32)
        G = jax.random.normal(ks[1], (H, E), dtype=jnp.float32)
        gate_w = jax.random.normal(ks[2], (E, F, H), dtype=jnp.float32) * np.float32(np.sqrt(2.0 / H))
        up_w = jax.random.normal(ks[3], (E, F, H), dtype=jnp.float32) * np.float32(np.sqrt(2.0 / H))
        down_w = jax.random.normal(ks[4], (E, H, F), dtype=jnp.float32) * np.float32(np.sqrt(2.0 / F))
        lora_A = jax.random.normal(ks[5], (E, LORA_R, H), dtype=jnp.float32) * np.float32(np.sqrt(2.0 / H))
        lora_B = jax.random.normal(ks[6], (E, H, LORA_R), dtype=jnp.float32) * np.float32(np.sqrt(2.0 / LORA_R))
        return {'x': x, 'G': G, 'gate_w': gate_w, 'up_w': up_w, 'down_w': down_w, 'lora_A': lora_A, 'lora_B': lora_B}
    _L0_ffn_all = _L0_ffn_setup()
    _L0_ffn_in = {k: v for k, v in _L0_ffn_all.items() if k in ('G', 'gate_w', 'up_w', 'down_w', 'lora_A', 'lora_B')}
    del _L0_ffn_all
    return {'x': x, 'ctx_2048': ctx_2048, 'mask_BxS2_bk0': mask_BxS2_bk0, 'L0_ffn_G': _L0_ffn_in['G'], 'L0_ffn_gate_w': _L0_ffn_in['gate_w'], 'L0_ffn_up_w': _L0_ffn_in['up_w'], 'L0_ffn_down_w': _L0_ffn_in['down_w'], 'L0_ffn_lora_A': _L0_ffn_in['lora_A'], 'L0_ffn_lora_B': _L0_ffn_in['lora_B']}

def reference(x, ctx_2048, mask_BxS2_bk0, L0_ffn_G, L0_ffn_gate_w, L0_ffn_up_w, L0_ffn_down_w, L0_ffn_lora_A, L0_ffn_lora_B):
    import jax
    import jax.numpy as jnp

    def _L0_xattn_ref(hidden_states, memory_tokens, memory_mask):
        import jax, jax.numpy as jnp
        import numpy as np
        B, S, D = hidden_states.shape
        scale = 1.0 / jnp.sqrt(jnp.asarray(D, hidden_states.dtype))
        scores = jnp.einsum('bsd,bmd->bsm', hidden_states, memory_tokens) * scale
        neg_inf = jnp.asarray(-1e+30, scores.dtype)
        scores = jnp.where(memory_mask[:, None, :], scores, neg_inf)
        attn = jax.nn.softmax(scores, axis=-1)
        readout = jnp.einsum('bsm,bmd->bsd', attn, memory_tokens)
        valid_b = jnp.any(memory_mask, axis=-1)
        out = jnp.where(valid_b[:, None, None], readout, jnp.zeros_like(readout))
        return out

    def _L0_ffn_ref(x, G, gate_w, up_w, down_w, lora_A, lora_B):
        import jax, jax.numpy as jnp
        import numpy as np
        B, S, H = (4, 512, 512)
        E = 8
        F = H // E
        TOPK = 2
        LORA_R = 16
        LORA_SCALE = 1.0
        scores = jax.nn.softmax(jnp.einsum('bsh,he->bse', x, G), axis=-1)
        value, indices = jax.lax.top_k(scores, TOPK)
        onehot = jax.nn.one_hot(indices, E, dtype=value.dtype)
        w = jnp.einsum('bsk,bske->bse', value, onehot)
        gate = jax.nn.silu(jnp.einsum('bsh,efh->bsef', x, gate_w))
        up = jnp.einsum('bsh,efh->bsef', x, up_w)
        gated = gate * up
        out = jnp.einsum('bsef,bse,ehf->bsh', gated, w, down_w)
        lr = jnp.einsum('bsh,erh->bser', x, lora_A)
        out = out + LORA_SCALE * jnp.einsum('bser,bse,ehr->bsh', lr, w, lora_B)
        return out
    x = x + _L0_xattn_ref(_layernorm(x, axis=-1), ctx_2048, mask_BxS2_bk0)
    x = x + _L0_ffn_ref(_layernorm(x, axis=-1), L0_ffn_G, L0_ffn_gate_w, L0_ffn_up_w, L0_ffn_down_w, L0_ffn_lora_A, L0_ffn_lora_B)
    return x

_drawn_inputs = setup_inputs


def setup_inputs(seed=0):
    import zlib

    import numpy as np

    out = dict(_drawn_inputs(seed))
    spreads = {}
    factors = {}
    for name, (base, spread) in spreads.items():
        noise = np.random.default_rng([zlib.crc32(name.encode()), seed]).standard_normal(out[name].shape)
        drawn = base * np.exp(spread * noise) if base else spread * noise
        out[name] = jnp.asarray(drawn.astype(out[name].dtype))
    for name, factor in factors.items():
        out[name] = (out[name] * factor).astype(out[name].dtype)
    return out
```

```python
from contextlib import ExitStack

import numpy as np
import concourse.bass as bass
from concourse import mybir

F32 = mybir.dt.float32
F32R = mybir.dt.float32r
U8 = mybir.dt.uint8
ALU = mybir.AluOpType
ACT = mybir.ActivationFunctionType
AX = mybir.AxisListType

B, S, D = 64, 128, 512
P = 128
KD = D // P
E, FE, R = 8, 64, 16
NB = 4
NG = B // NB
T = NB * S
NC = E * FE // P
NU = 2 * NC + NB
LR = E * R
GA = E + LR
SCALE = float(D) ** -0.5
EPS = 1e-5
BIG = 1e30
RING = 3
LAST_R, FIRST_S = 9, 3


def past(count, least):
    return not isinstance(count, int) or count >= least


def xattn_moe(nc, x, ctx, ctxT, mask, wgu, ga, dn, consts, out):
    with ExitStack() as stack:
        def sb(name, shape, dt=F32):
            return stack.enter_context(nc.sbuf_tensor(name, [P] + shape, dt))

        def sem(name):
            return stack.enter_context(nc.semaphore(name))

        def bank(name):
            return stack.enter_context(nc.psum_tensor(name, [P, 512], F32))
        ffn_ps = [bank(f"ffn_ps{i}") for i in range(RING)]
        w_ps = bank("w_ps")
        xnT_ps = bank("xnT_ps")
        sr_ps = bank("sr_ps")
        pv_ps = bank("pv_ps")
        h2T_ps = bank("h2T_ps")

        wgu_raw = sb("wgu_raw", [KD // 2, 2 * E * FE])
        wgu_hi, wgu_lo = sb("wgu_hi", [KD, 2 * E * FE], F32R), sb("wgu_lo", [KD, 2 * E * FE], F32R)
        ga_raw = sb("ga_raw", [KD, GA])
        ga_r = sb("ga_r", [KD, 2 * GA], F32R)
        dn_raw = sb("dn_raw", [NC + 1, D])
        dn_hi, dn_lo = sb("dn_hi", [NC + 1, D], F32R), sb("dn_lo", [NC + 1, D], F32R)
        const_sb = sb("const_sb", [NC * P + P + NB * E * E])
        sel = sb("sel", [NC, P], F32R)
        ident = const_sb[:, NC * P:NC * P + P]
        earlier = const_sb[:, NC * P + P:].rearrange("p (b e f) -> p b e f", b=NB, e=E)
        nhalf = sb("nhalf", [1])

        x_sb = sb("x_sb", [NB, D])
        ctx_sb = sb("ctx_sb", [NB, D])
        ctxT_sb = sb("ctxT_sb", [NB, KD, P])
        mask_sb = sb("mask_sb", [NB, S], U8)
        bias = sb("bias", [NB, S])
        valid = sb("valid", [NB])
        xn = sb("xn", [2, D])
        xnT = sb("xnT", [KD, P])
        masked = sb("masked", [S])
        rowmax, negmax = sb("rowmax", [1]), sb("negmax", [1])
        prob, rowsum = sb("prob", [S]), sb("rowsum", [1])
        rinv, rinv_v = sb("rinv", [1]), sb("rinv_v", [1])
        pT_hi, pT_lo = sb("pT_hi", [S], F32R), sb("pT_lo", [S], F32R)
        ctx_hi, ctx_lo = sb("ctx_hi", [D], F32R), sb("ctx_lo", [D], F32R)
        x1 = sb("x1", [2, NB, D])
        h2 = sb("h2", [D])
        st1, mv1, ln1 = sb("st1", [6]), sb("mv1", [2]), sb("ln1", [3])
        st2, mv2, ln2 = sb("st2", [6]), sb("mv2", [2]), sb("ln2", [3])

        h2T_hi, h2T_lo = sb("h2T_hi", [2, KD, T], F32R), sb("h2T_lo", [2, KD, T], F32R)
        router = sb("router", [NB, GA])
        lmax, lexp, lsum, linv = sb("lmax", [NB]), sb("lexp", [NB, E]), sb("lsum", [NB]), sb("linv", [NB])
        gt, eq = sb("gt", [NB, E, E]), sb("eq", [NB, E, E])
        rank, rw = sb("rank", [NB, E]), sb("rw", [NB, E])
        whi = sb("whi", [NB, E], F32R)
        wpad = sb("wpad", [NB, P])
        lrw = sb("lrw", [NB, LR])
        wT = sb("wT", [T], F32R)
        th, t1, gw = sb("th", [T]), sb("t1", [T]), sb("gw", [T])
        gat_hi, gat_lo = sb("gat_hi", [NC + 1, T], F32R), sb("gat_lo", [NC + 1, T], F32R)

        wgu_loaded = [sem("wgu_loaded0"), sem("wgu_loaded1")]
        ga_loaded, dn_loaded, const_loaded = map(sem, ("ga_loaded", "dn_loaded", "const_loaded"))
        x_loaded = [sem(f"x_loaded{b}") for b in range(NB)]
        ctx_loaded = [sem(f"ctx_loaded{b}") for b in range(NB)]
        ctxT_loaded = [sem(f"ctxT_loaded{b}") for b in range(NB)]
        mask_loaded = sem("mask_loaded")
        stored = [sem(f"stored{b}") for b in range(NB)]
        w_hi_ready, w_ready = sem("w_hi_ready"), sem("w_ready")
        set_up = sem("set_up")
        bias_ready, valid_ready = sem("bias_ready"), sem("valid_ready")
        st1_done, mv1_ready, ln1_step, xn_ready = map(sem, ("st1_done", "mv1_ready", "ln1_step", "xn_ready"))
        st2_done, mv2_ready, ln2_step, h2_ready = map(sem, ("st2_done", "mv2_ready", "ln2_step", "h2_ready"))
        xnT_done, xnT_ready = sem("xnT_done"), sem("xnT_ready")
        scores_done, masked_ready, negmax_ready, prob_ready = map(sem, ("scores_done", "masked_ready", "negmax_ready", "prob_ready"))
        rinv_step, pT_done, pT_hi_ready, pT_lo_ready = map(sem, ("rinv_step", "pT_done", "pT_hi_ready", "pT_lo_ready"))
        ctx_hi_ready, ctx_lo_ready = sem("ctx_hi_ready"), sem("ctx_lo_ready")
        pv_done, x1_ready = sem("pv_done"), sem("x1_ready")
        h2T_done, h2T_hi_ready, h2T_lo_ready = map(sem, ("h2T_done", "h2T_hi_ready", "h2T_lo_ready"))
        router_done, lr_ready = sem("router_done"), sem("lr_ready")
        rt, lexp_ready, rw_ready = sem("rt"), sem("lexp_ready"), sem("rw_ready")
        wT_done, wT_ready = sem("wT_done"), sem("wT_ready")
        lrT_done, lr_hi_ready, lr_lo_ready = map(sem, ("lrT_done", "lr_hi_ready", "lr_lo_ready"))
        gate_up_done = sem("gate_up_done")
        th_ready, t1_ready, t2_ready, wb_done, gw_ready, gat_hi_ready, gat_lo_ready = map(
            sem, ("th_ready", "t1_ready", "t2_ready", "wb_done", "gw_ready", "gat_hi_ready", "gat_lo_ready"))
        down_done, out_ready = sem("down_done"), sem("out_ready")
        sp_waited, dve_waited, pool_waited = sem("sp_waited"), sem("dve_waited"), sem("pool_waited")
        RT = 13
        LEAD, LEAD0 = 1, 2

        def wgu_part(k):
            half = k - KD // 2
            return wgu_raw[:, k, :] if half < 0 else x1[:, 1, :, :].rearrange("p b d -> p (b d)")[:, half * 2 * E * FE:(half + 1) * 2 * E * FE]

        block = stack.enter_context(nc.Block())

        def steps(engine, step):
            step(0, 0, True, True)
            with engine.Fori(0, (NG - 4) // 2) as i:
                step(2 * i + 1, 1, True, True)
                step(2 * i + 2, 0, True, True)
            step(NG - 3, 1, True, True)
            step(NG - 2, 0, True, False)
            step(NG - 1, 1, False, False)

        @block.sync
        def _(sp):
            def load(g, b):
                sp.dma_start(x_sb[:, b, :], x[NB * g + b]).then_inc(x_loaded[b], 16)
                sp.dma_start(ctxT_sb[:, b, :, :], ctxT[NB * g + b]).then_inc(ctxT_loaded[b], 16)
                sp.dma_start(ctx_sb[:, b, :], ctx[NB * g + b]).then_inc(ctx_loaded[b], 16)

            def load_mask(g):
                sp.dma_start(mask_sb[:], mask[g].partition_broadcast(P)).then_inc(mask_loaded, 16)

            load_mask(0)
            load(0, 0)
            sp.dma_start(const_sb[:], consts).then_inc(const_loaded, 16)
            sp.dma_start(ga_raw[:], ga).then_inc(ga_loaded, 16)
            load(0, 1)
            sp.dma_start(wgu_raw[:], wgu[:, 0:KD // 2, :]).then_inc(wgu_loaded[0], 16)
            load(0, 2)
            sp.dma_start(x1[:, 1, :, :].rearrange("p b d -> p (b d)"),
                         wgu[:, KD // 2:, :].rearrange("p k f -> p (k f)")).then_inc(wgu_loaded[1], 16)
            load(0, 3)
            sp.dma_start(dn_raw[:], dn).then_inc(dn_loaded, 16)

            def step(g, p, attn, more):
                a = g + 1
                if more:
                    sp.wait_ge(bias_ready, a + 1)
                    sp.wait_ge(valid_ready, a + 1)
                    sp.sem_inc(sp_waited, 1)
                    load_mask(a + 1)
                    for b in range(NB):
                        n = NB * a + b
                        sp.wait_ge(x1_ready, n + 1)
                        sp.wait_ge(scores_done, n + 1)
                        sp.wait_ge(ctx_lo_ready, n + 1)
                        sp.sem_inc(sp_waited, 1)
                        load(a + 1, b)
                if past(g, 0):
                    for b in range(NB):
                        sp.wait_ge(out_ready, NB * g + b + 1)
                        sp.sem_inc(sp_waited, 1)
                        sp.dma_start(out[NB * g + b], x1[:, p, b, :]).then_inc(stored[b], 16)

            step(-1, 1, True, True)
            steps(sp, step)
            for b in range(NB):
                sp.wait_ge(stored[b], 16 * NG)

        @block.tensor
        def _(pe):
            def three(psum, hi, lo, x_hi, x_lo, start, stop):
                pe.matmul(psum, hi, x_hi, start=start, stop=False)
                pe.matmul(psum, hi, x_lo, start=False, stop=False)
                return pe.matmul(psum, lo, x_hi, start=False, stop=stop)

            def turn_xn(a, b):
                n = NB * a + b
                pe.wait_ge(xn_ready, n + 1)
                if past(n, 1):
                    pe.wait_ge(xnT_ready, n)
                for k in range(KD):
                    mm = pe.transpose(xnT_ps[:, k * P:(k + 1) * P], xn[:, b % 2, k * P:(k + 1) * P], ident)
                mm.then_inc(xnT_done, 1)

            def scores(a, b, lead=LEAD):
                n = NB * a + b
                pe.wait_ge(xnT_ready, n + 1)
                pe.wait_ge(ctxT_loaded[b], 16 * (a + 1))
                if past(n, 1):
                    pe.wait_ge(masked_ready, n)
                if (b == 0 and past(n, 1)) or b > lead:
                    pe.wait_ge(lr_ready, n if b == 0 else n - lead)
                for k in range(KD):
                    mm = pe.matmul(sr_ps[:, 0:S], xnT[:, k, :], ctxT_sb[:, b, k, :], start=(k == 0), stop=(k == KD - 1))
                mm.then_inc(scores_done, 1)

            def turn_prob(a, b):
                n = NB * a + b
                pe.wait_ge(prob_ready, n + 1)
                if past(n, 1):
                    pe.wait_ge(x1_ready, n)
                if b == 0 and past(a, 1):
                    pe.wait_ge(lr_lo_ready, a)
                pe.transpose(pv_ps[:, 0:S], prob[:], ident).then_inc(pT_done, 1)

            def readout(a, b):
                n = NB * a + b
                pe.wait_ge(pT_lo_ready, n + 1)
                pe.wait_ge(ctx_lo_ready, n + 1)
                three(pv_ps[:], pT_hi[:], pT_lo[:], ctx_hi[:], ctx_lo[:], True, True).then_inc(pv_done, 1)

            def turn_h2(a, b):
                n = NB * a + b
                pe.wait_ge(h2_ready, n + 1)
                if past(n, 1):
                    pe.wait_ge(h2T_lo_ready, n)
                for k in range(KD):
                    mm = pe.transpose(h2T_ps[:, k * P:(k + 1) * P], h2[:, k * P:(k + 1) * P], ident)
                mm.then_inc(h2T_done, 1)

            def route(a, q, b, lead=LEAD):
                n = NB * a + b
                if b == 0 and not past(n, 1):
                    pe.wait_ge(w_ready, 1)
                pe.wait_ge(h2T_lo_ready, n + 1)
                pe.wait_ge(masked_ready, n + 1 + min(lead, NB - 1 - b))
                for k in range(KD):
                    pe.matmul(sr_ps[:, 0:2 * GA], h2T_hi[:, q, k, b * S:(b + 1) * S], ga_r[:, k, :], start=(k == 0), stop=False)
                    mm = pe.matmul(sr_ps[:, 0:2 * GA], h2T_lo[:, q, k, b * S:(b + 1) * S], ga_r[:, k, :], start=False, stop=(k == KD - 1))
                mm.then_inc(router_done, 1)

            def turn_weights(g):
                pe.wait_ge(rw_ready, g + 1)
                if past(g, 1):
                    pe.wait_ge(gw_ready, NC * g)
                for b in range(NB):
                    mm = pe.transpose(w_ps[:, b * S:(b + 1) * S], wpad[:, b, :], ident)
                mm.then_inc(wT_done, 1)
                pe.wait_ge(x1_ready, NB * g + NB)
                for b in range(NB):
                    mm = pe.transpose(pv_ps[:, b * S:(b + 1) * S], lrw[:, b, :], ident)
                mm.then_inc(lrT_done, 1)

            def spread(g, c):
                if c == 0:
                    pe.wait_ge(wT_ready, g + 1)
                else:
                    pe.wait_ge(gw_ready, NC * g + c)
                pe.matmul(w_ps[:], sel[:, c, :], wT[:], start=True, stop=True).then_inc(wb_done, 1)

            def ffn_unit(g, p, u, between):
                ps = ffn_ps[u % RING]
                v = u - RING
                if v < 0:
                    if past(g, 1):
                        pe.wait_ge(out_ready, NB * g + v + 1)
                elif v >= 2 * NC:
                    pe.wait_ge(out_ready, NB * g + v - 2 * NC + 1)
                elif v % 2 == 0:
                    pe.wait_ge(t1_ready, NC * g + v // 2 + 1)
                else:
                    pe.wait_ge(t2_ready, NC * g + v // 2 + 1)
                if u < 2 * NC:
                    c, col = u // 2, (u % 2) * E * FE + (u // 2) * P
                    if u == 0:
                        pe.wait_ge(h2T_lo_ready, NB * g + NB)
                        if not past(g, 1):
                            pe.wait_ge(w_ready, KD + 1)
                    for k in range(KD):
                        if 3 * k == (FIRST_S if u % 2 else LAST_R):
                            between()
                        mm = three(ps[:], wgu_hi[:, k, col:col + P], wgu_lo[:, k, col:col + P],
                                   h2T_hi[:, p, k, :], h2T_lo[:, p, k, :], k == 0, k == KD - 1)
                    mm.then_inc(gate_up_done, 1)
                else:
                    b = u - 2 * NC
                    if b == 0:
                        if not past(g, 1):
                            pe.wait_ge(w_ready, KD + 2)
                        pe.wait_ge(lr_lo_ready, g + 1)
                    order = [NC] + list(range(NC))
                    for j, c in enumerate(order):
                        if 3 * j == LAST_R:
                            between()
                        if b == 0 and c < NC:
                            pe.wait_ge(gat_lo_ready, NC * g + c + 1)
                        tok = slice(b * S, (b + 1) * S)
                        hi, lo, w_hi, w_lo = gat_hi[:, c, tok], gat_lo[:, c, tok], dn_hi[:, c, :], dn_lo[:, c, :]
                        mm = three(ps[:], hi, lo, w_hi, w_lo, j == 0, j == NC)
                    mm.then_inc(down_done, 1)

            def step(g, p, attn, more):
                a, q = g + 1, 1 - p
                for u in range(NU):
                    k, even = u // 2, u % 2 == 0
                    if attn and even and k < NB:
                        turn_xn(a, k)
                    if attn and even and 1 <= k <= NB:
                        turn_prob(a, k - 1)

                    def between():
                        if attn and even and 1 <= k <= NB:
                            readout(a, k - 1)
                        if attn and even and 2 <= k < NB + 2:
                            route(a, q, k - 2)
                        if attn and not even and k < NB:
                            scores(a, k)
                    ffn_unit(g, p, u, between)
                    if u == 0:
                        turn_weights(g)
                    if not even and k < NC:
                        spread(g, k)
                    if attn and not even and 1 <= k <= NB:
                        turn_h2(a, k - 1)

            def first():
                turn_xn(0, 0)
                for k in range(NB + 2):
                    if k < NB:
                        scores(0, k, LEAD0)
                    if 1 <= k <= NB:
                        turn_prob(0, k - 1)
                    if k < NB - 1:
                        turn_xn(0, k + 1)
                    if k >= 2:
                        turn_h2(0, k - 2)
                    if 1 <= k <= NB:
                        readout(0, k - 1)
                    if k >= 2:
                        route(0, 0, k - 2, LEAD0)

            pe.wait_ge(const_loaded, 16)
            first()
            steps(pe, step)

        @block.scalar
        def _(act):
            def normalise_x(a, b):
                n = NB * a + b
                act.wait_ge(ln1_step, 3 * n + 3)
                if past(n, 2):
                    act.wait_ge(xnT_done, n - 1)
                act.activation(xn[:, b % 2, :], x_sb[:, b, :], ACT.Identity, scale=ln1[:, 1:2], bias=ln1[:, 2:3]).then_inc(xn_ready, 1)

            def keep_h2T(a, g, q, b):
                n = NB * a + b
                act.wait_ge(h2T_done, n + 1)
                if b == 0 and past(g, 1):
                    act.wait_ge(gate_up_done, 2 * NC * g)
                act.copy(h2T_hi[:, q, :, b * S:(b + 1) * S], h2T_ps[:].rearrange("p (k s) -> p k s", k=KD)).then_inc(h2T_hi_ready, 1)

            def keep_xnT(a, b):
                n = NB * a + b
                act.wait_ge(xnT_done, n + 1)
                if past(n, 1):
                    act.wait_ge(scores_done, n)
                act.copy(xnT[:].rearrange("p k s -> p (k s)"), xnT_ps[:]).then_inc(xnT_ready, 1)

            def keep_pT(a, b):
                n = NB * a + b
                act.wait_ge(pT_done, n + 1)
                if past(n, 1):
                    act.wait_ge(pv_done, n)
                act.copy(pT_hi[:], pv_ps[:, 0:S]).then_inc(pT_hi_ready, 1)

            def split_gated(g, c):
                act.wait_ge(gw_ready, NC * g + c + 1)
                if c == 0 and past(g, 1):
                    act.wait_ge(down_done, NB * g)
                act.copy(gat_hi[:, c, :], gw[:]).then_inc(gat_hi_ready, 1)

            def half_tanh(g, c):
                act.wait_ge(gate_up_done, 2 * NC * g + 2 * c + 1)
                if c or past(g, 1):
                    act.wait_ge(t1_ready, NC * g + c)
                act.activation(th[:], ffn_ps[2 * c % RING][:], ACT.Tanh, scale=0.5).then_inc(th_ready, 1)

            def keep_weights(g):
                act.wait_ge(wT_done, g + 1)
                if past(g, 1):
                    act.wait_ge(wb_done, NC * g)
                act.copy(wT[:], w_ps[:]).then_inc(wT_ready, 1)

            def keep_lrT(g):
                act.wait_ge(lrT_done, g + 1)
                if past(g, 1):
                    act.wait_ge(down_done, NB * g)
                act.copy(gat_hi[:, NC, :], pv_ps[:]).then_inc(lr_hi_ready, 1)

            def softmax_exp(a, b):
                n = NB * a + b
                act.wait_ge(negmax_ready, n + 1)
                if past(n, 1):
                    act.wait_ge(pT_done, n)
                    act.wait_ge(rinv_step, 2 * n)
                act.activation(prob[:], masked[:], ACT.Exp, bias=negmax[:], accum_out=rowsum[:]).then_inc(prob_ready, 1)

            def split_ctx(a, b):
                n = NB * a + b
                act.wait_ge(ctx_loaded[b], 16 * (a + 1))
                if past(n, 1):
                    act.wait_ge(pv_done, n)
                act.copy(ctx_hi[:], ctx_sb[:, b, :]).then_inc(ctx_hi_ready, 1)

            def normalise_x1(a, b, p):
                n = NB * a + b
                act.wait_ge(ln2_step, 3 * n + 3)
                if past(n, 1):
                    act.wait_ge(h2T_done, n)
                act.activation(h2[:], x1[:, 1 - p, b, :], ACT.Identity, scale=ln2[:, 1:2], bias=ln2[:, 2:3]).then_inc(h2_ready, 1)

            def router_exp(a):
                act.wait_ge(rt, RT * a + 2)
                act.activation(lexp[:], lexp[:], ACT.Exp).then_inc(lexp_ready, 1)

            def step(g, p, attn, more):
                a, q = g + 1, 1 - p
                for u in range(NU):
                    k, even = u // 2, u % 2 == 0
                    if even:
                        if attn and 2 <= k < NB + 2:
                            keep_h2T(a, g, q, k - 2)
                        if attn and 1 <= k <= NB:
                            keep_pT(a, k - 1)
                        if attn and k < NB:
                            keep_xnT(a, k)
                        if 1 <= k <= NC:
                            split_gated(g, k - 1)
                        if k < NC:
                            half_tanh(g, k)
                        if attn and k == NB + 1:
                            router_exp(a)
                        if attn and k < NB - 1:
                            normalise_x(a, k + 1)
                        if more and k == NB + 1:
                            normalise_x(a + 1, 0)
                    else:
                        if k == 0:
                            keep_weights(g)
                        if attn and k < NB:
                            split_ctx(a, k)
                            softmax_exp(a, k)
                        if k == 0:
                            keep_lrT(g)
                        if attn and 1 <= k <= NB:
                            normalise_x1(a, k - 1, p)

            def weights_hi(k):
                if k == 0:
                    act.wait_ge(ga_loaded, 16)
                    act.copy(ga_r[:, :, 0:GA], ga_raw[:]).then_inc(w_hi_ready, 1)
                elif k <= KD:
                    act.wait_ge(wgu_loaded[(k - 1) // (KD // 2)], 16)
                    act.copy(wgu_hi[:, k - 1, :], wgu_part(k - 1)).then_inc(w_hi_ready, 1)
                else:
                    act.wait_ge(dn_loaded, 16)
                    act.copy(dn_hi[:], dn_raw[:]).then_inc(w_hi_ready, 1)

            def first():
                normalise_x(0, 0)
                keep_xnT(0, 0)
                normalise_x(0, 1)
                for k in range(NB + 2):
                    if k >= 2:
                        normalise_x1(0, k - 2, 1)
                    if 1 <= k <= NB:
                        keep_pT(0, k - 1)
                    if k < NB:
                        softmax_exp(0, k)
                    if k < NB - 1:
                        keep_xnT(0, k + 1)
                    if k >= 2:
                        keep_h2T(0, -1, 0, k - 2)
                    if k < NB - 2:
                        normalise_x(0, k + 2)
                    if k < NB:
                        split_ctx(0, k)
                    weights_hi(k)
                router_exp(0)
                normalise_x(1, 0)

            first()
            steps(act, step)

        @block.vector
        def _(dve):
            def stats_x(a, b):
                n = NB * a + b
                dve.wait_ge(x_loaded[b], 16 * (a + 1))
                if past(n, 1):
                    dve.wait_ge(mv1_ready, n)
                dve.bn_stats(st1[:], x_sb[:, b, :]).then_inc(st1_done, 1)
                dve.wait_ge(st1_done, n + 1)
                if past(n, 1):
                    dve.wait_ge(ln1_step, 3 * n)
                dve.sem_inc(dve_waited, 1)
                dve.bn_aggr(mv1[:], st1[:]).then_inc(mv1_ready, 1)

            def stats_x1(a, b, q):
                n = NB * a + b
                dve.wait_ge(x1_ready, n + 1)
                if past(n, 1):
                    dve.wait_ge(mv2_ready, n)
                dve.bn_stats(st2[:], x1[:, q, b, :]).then_inc(st2_done, 1)
                dve.wait_ge(st2_done, n + 1)
                if past(n, 1):
                    dve.wait_ge(ln2_step, 3 * n)
                dve.sem_inc(dve_waited, 1)
                dve.bn_aggr(mv2[:], st2[:]).then_inc(mv2_ready, 1)

            def any_valid(a):
                dve.wait_ge(mask_loaded, 16 * (a + 1))
                if past(a, 1):
                    dve.wait_ge(rinv_step, 2 * NB * a)
                dve.tensor_reduce(valid[:], mask_sb[:], AX.X, ALU.max).then_inc(valid_ready, 1)

            def split_pT(a, b):
                n = NB * a + b
                dve.wait_ge(pT_hi_ready, n + 1)
                dve.tensor_tensor(pT_lo[:], pv_ps[:, 0:S], pT_hi[:].bitcast(F32), ALU.subtract).then_inc(pT_lo_ready, 1)

            def split_h2T(a, q, b):
                n = NB * a + b
                dve.wait_ge(h2T_hi_ready, n + 1)
                dve.tensor_tensor(h2T_lo[:, q, :, b * S:(b + 1) * S], h2T_ps[:].rearrange("p (k s) -> p k s", k=KD),
                                  h2T_hi[:, q, :, b * S:(b + 1) * S].bitcast(F32), ALU.subtract).then_inc(h2T_lo_ready, 1)

            def gated_times_weight(g, c):
                m = NC * g + c
                dve.wait_ge(gate_up_done, 2 * NC * g + 2 * c + 2)
                dve.wait_ge(t1_ready, m + 1)
                dve.tensor_tensor(t1[:], t1[:], ffn_ps[(2 * c + 1) % RING][:], ALU.mult).then_inc(t2_ready, 1)
                dve.wait_ge(wb_done, m + 1)
                dve.wait_ge(t2_ready, m + 1)
                if c or past(g, 1):
                    dve.wait_ge(gat_lo_ready, m)
                dve.tensor_tensor(gw[:], t1[:], w_ps[:], ALU.mult).then_inc(gw_ready, 1)

            def router_sums(a, b):
                n = NB * a + b
                dve.wait_ge(router_done, n + 1)
                dve.tensor_reduce(router[:, b, :], sr_ps[:, 0:2 * GA].rearrange("p (part f) -> p f part", part=2),
                                  AX.X, ALU.add).then_inc(lr_ready, 1)

            def gate_times_up(g, c):
                dve.wait_ge(th_ready, NC * g + c + 1)
                dve.scalar_tensor_tensor(out=t1[:], in0=th[:], scalar=1.0, in1=ffn_ps[2 * c % RING][:],
                                         op0=ALU.add, op1=ALU.mult).then_inc(t1_ready, 1)

            def row_weights(a, b):
                n = NB * a + b
                dve.wait_ge(prob_ready, n + 1)
                if past(n, 1):
                    dve.wait_ge(x1_ready, n)
                dve.reciprocal(rinv[:], rowsum[:]).then_inc(rinv_step, 1)
                dve.wait_ge(rinv_step, 2 * n + 1)
                if b == 0:
                    dve.wait_ge(valid_ready, a + 1)
                dve.tensor_tensor(rinv_v[:], rinv[:], valid[:, b:b + 1], ALU.mult).then_inc(rinv_step, 1)

            def add_readout(a, q, b):
                n = NB * a + b
                dve.wait_ge(rinv_step, 2 * n + 2)
                dve.wait_ge(pv_done, n + 1)
                if b == 0 and q == 1 and not past(a, 2):
                    dve.wait_ge(w_ready, KD + 1)
                if past(a, 2):
                    dve.wait_ge(stored[b], 16 * (a - 1))
                dve.scalar_tensor_tensor(out=x1[:, q, b, :], in0=pv_ps[:], scalar=rinv_v[:], in1=x_sb[:, b, :],
                                         op0=ALU.mult, op1=ALU.add).then_inc(x1_ready, 1)

            def mask_scores(a, b):
                n = NB * a + b
                dve.wait_ge(scores_done, n + 1)
                if b == 0:
                    dve.wait_ge(bias_ready, a + 1)
                if past(n, 1):
                    dve.wait_ge(prob_ready, n)
                dve.sem_inc(dve_waited, 1)
                dve.tensor_tensor_reduce(masked[:], sr_ps[:, 0:S], bias[:, b, :], SCALE, -3e38, ALU.add, ALU.max,
                                         rowmax[:]).then_inc(masked_ready, 1)
                dve.wait_ge(masked_ready, n + 1)
                dve.tensor_scalar(negmax[:], rowmax[:], -1.0, None, ALU.mult).then_inc(negmax_ready, 1)

            def add_ffn(g, p, b):
                dve.wait_ge(down_done, NB * g + b + 1)
                dve.tensor_tensor(x1[:, p, b, :], ffn_ps[(2 * NC + b) % RING][:], x1[:, p, b, :], ALU.add).then_inc(out_ready, 1)

            def split_lr(g):
                dve.wait_ge(lr_hi_ready, g + 1)
                dve.tensor_tensor(gat_lo[:, NC, :], pv_ps[:], gat_hi[:, NC, :].bitcast(F32), ALU.subtract).then_inc(lr_lo_ready, 1)

            def route(a):
                def over(v):
                    return v.rearrange("p (b o) -> p b o", o=1).broadcast_to([P, NB, E])
                s = RT * a
                logits, lr = router[:, :, 0:E], router[:, :, E:]
                dve.wait_ge(lr_ready, NB * a + NB)
                dve.tensor_reduce(lmax[:], logits, AX.X, ALU.max).then_inc(rt, 1)
                dve.wait_ge(rt, s + 1)
                dve.tensor_tensor(lexp[:], logits, over(lmax[:]), ALU.subtract).then_inc(rt, 1)
                dve.wait_ge(lexp_ready, a + 1)
                dve.tensor_reduce(lsum[:], lexp[:], AX.X, ALU.add).then_inc(rt, 1)
                dve.wait_ge(rt, s + 3)
                dve.reciprocal(linv[:], lsum[:]).then_inc(rt, 1)
                dve.wait_ge(rt, s + 4)
                dve.tensor_tensor(lexp[:], lexp[:], over(linv[:]), ALU.mult).then_inc(rt, 1)
                dve.wait_ge(rt, s + 5)
                own = lexp[:].rearrange("p b (e o) -> p b e o", o=1).broadcast_to([P, NB, E, E])
                other = lexp[:].rearrange("p b (o e) -> p b o e", o=1).broadcast_to([P, NB, E, E])
                dve.tensor_tensor(gt[:], other, own, ALU.is_gt).then_inc(rt, 1)
                dve.tensor_tensor(eq[:], other, own, ALU.is_equal).then_inc(rt, 1)
                dve.wait_ge(rt, s + 7)
                dve.tensor_tensor(eq[:], eq[:], earlier, ALU.mult).then_inc(rt, 1)
                dve.wait_ge(rt, s + 8)
                dve.tensor_tensor(gt[:], gt[:], eq[:], ALU.add).then_inc(rt, 1)
                dve.wait_ge(rt, s + 9)
                dve.tensor_reduce(rank[:], gt[:], AX.X, ALU.add).then_inc(rt, 1)
                dve.wait_ge(rt, s + 10)
                dve.scalar_tensor_tensor(out=rw[:], in0=rank[:], scalar=1.5, in1=lexp[:], op0=ALU.is_lt, op1=ALU.mult).then_inc(rt, 1)
                dve.wait_ge(rt, s + 11)
                if past(a, 1):
                    dve.wait_ge(lrT_done, a)
                dve.tensor_scalar(whi[:], rw[:], 0.5, None, ALU.mult).then_inc(rt, 1)
                dve.wait_ge(rt, s + 12)
                dve.tensor_copy(wpad[:, :, 0:E], whi[:].bitcast(F32)).then_inc(rt, 1)
                dve.scalar_tensor_tensor(out=wpad[:, :, E:2 * E], in0=rw[:], scalar=0.5, in1=whi[:].bitcast(F32),
                                         op0=ALU.mult, op1=ALU.subtract)
                dve.tensor_tensor(lrw[:].rearrange("p b (e r) -> p b e r", e=E), lr.rearrange("p b (e r) -> p b e r", e=E),
                                  rw[:].rearrange("p b (e o) -> p b e o", o=1).broadcast_to([P, NB, E, R]),
                                  ALU.mult).then_inc(rw_ready, 1)

            def step(g, p, attn, more):
                a, q = g + 1, 1 - p
                for u in range(NU):
                    k, even = u // 2, u % 2 == 0
                    if even:
                        if 1 <= k <= NC:
                            gated_times_weight(g, k - 1)
                        if attn and 1 <= k <= NB:
                            row_weights(a, k - 1)
                            split_pT(a, k - 1)
                        if attn and 2 <= k < NB + 2:
                            split_h2T(a, q, k - 2)
                        if k == NC + 1:
                            add_ffn(g, p, 1)
                        if attn and 1 <= k <= NB:
                            add_readout(a, q, k - 1)
                        if attn and 2 <= k < NB + 2:
                            router_sums(a, k - 2)
                        if attn and 1 <= k <= NB:
                            stats_x1(a, k - 1, q)
                        if attn and k == NB + 1:
                            route(a)
                    else:
                        if attn and k < NB:
                            mask_scores(a, k)
                        if k < NC:
                            gate_times_up(g, k)
                        if k == 0:
                            split_lr(g)
                        if attn and k < NB - 2:
                            stats_x(a, k + 2)
                        if k == NC:
                            add_ffn(g, p, 0)
                        if more and k == NB:
                            any_valid(a + 1)
                        if more and k >= NB:
                            stats_x(a + 1, k - NB)
                        if k == NC + 1:
                            add_ffn(g, p, 2)
                            add_ffn(g, p, 3)

            def weights_lo(k):
                dve.wait_ge(w_hi_ready, k + 1)
                if k == 0:
                    dve.wait_ge(const_loaded, 16)
                    dve.tensor_copy(sel[:], const_sb[:, 0:NC * P].rearrange("p (c f) -> p c f", c=NC))
                    dve.tensor_tensor(ga_r[:, :, GA:], ga_raw[:], ga_r[:, :, 0:GA].bitcast(F32), ALU.subtract).then_inc(w_ready, 1)
                elif k <= KD:
                    dve.tensor_tensor(wgu_lo[:, k - 1, :], wgu_part(k - 1), wgu_hi[:, k - 1, :].bitcast(F32),
                                      ALU.subtract).then_inc(w_ready, 1)
                else:
                    dve.tensor_tensor(dn_lo[:], dn_raw[:], dn_hi[:].bitcast(F32), ALU.subtract).then_inc(w_ready, 1)

            def first():
                stats_x(0, 0)
                stats_x(0, 1)
                any_valid(0)
                dve.memset(wpad[:], 0.0)
                for k in range(NB + 2):
                    if k < NB:
                        mask_scores(0, k)
                    if 1 <= k <= NB:
                        row_weights(0, k - 1)
                        split_pT(0, k - 1)
                    if k < NB - 2:
                        stats_x(0, k + 2)
                    if k >= 2:
                        split_h2T(0, 0, k - 2)
                    if 1 <= k <= NB:
                        add_readout(0, 0, k - 1)
                        stats_x1(0, k - 1, 0)
                    if k >= 2:
                        router_sums(0, k - 2)
                    if k >= NB:
                        stats_x(1, k - NB)
                    if k <= NB:
                        weights_lo(k)
                any_valid(1)
                route(0)
                weights_lo(NB + 1)

            first()
            steps(dve, step)

        @block.gpsimd
        def _(pool):
            def rstd_x(a, b):
                n = NB * a + b
                pool.wait_ge(mv1_ready, n + 1)
                if past(n, 1):
                    pool.wait_ge(xn_ready, n)
                pool.sem_inc(pool_waited, 1)
                pool.tensor_scalar(ln1[:, 0:1], mv1[:, 1:2], EPS, None, ALU.add).then_inc(ln1_step, 1)
                pool.wait_ge(ln1_step, 3 * n + 1)
                pool.tensor_tensor(ln1[:, 1:2], ln1[:, 0:1], nhalf[:], ALU.pow).then_inc(ln1_step, 1)
                pool.wait_ge(ln1_step, 3 * n + 2)
                pool.sem_inc(pool_waited, 1)
                pool.tensor_scalar(ln1[:, 2:3], mv1[:, 0:1], ln1[:, 1:2], -1.0, ALU.mult, ALU.mult).then_inc(ln1_step, 1)

            def rstd_x1(a, b):
                n = NB * a + b
                pool.wait_ge(mv2_ready, n + 1)
                if past(n, 1):
                    pool.wait_ge(h2_ready, n)
                pool.sem_inc(pool_waited, 1)
                pool.tensor_scalar(ln2[:, 0:1], mv2[:, 1:2], EPS, None, ALU.add).then_inc(ln2_step, 1)
                pool.wait_ge(ln2_step, 3 * n + 1)
                pool.tensor_tensor(ln2[:, 1:2], ln2[:, 0:1], nhalf[:], ALU.pow).then_inc(ln2_step, 1)
                pool.wait_ge(ln2_step, 3 * n + 2)
                pool.sem_inc(pool_waited, 1)
                pool.tensor_scalar(ln2[:, 2:3], mv2[:, 0:1], ln2[:, 1:2], -1.0, ALU.mult, ALU.mult).then_inc(ln2_step, 1)

            def mask_bias(a):
                pool.wait_ge(mask_loaded, 16 * (a + 1))
                if past(a, 1):
                    pool.wait_ge(masked_ready, NB * a)
                pool.sem_inc(pool_waited, 1)
                pool.tensor_scalar(bias[:], mask_sb[:], BIG, -BIG, ALU.mult, ALU.add).then_inc(bias_ready, 1)

            def split_ctx(a, b):
                n = NB * a + b
                pool.wait_ge(ctx_hi_ready, n + 1)
                pool.tensor_tensor(ctx_lo[:], ctx_sb[:, b, :], ctx_hi[:].bitcast(F32), ALU.subtract).then_inc(ctx_lo_ready, 1)

            def split_gated(g, c):
                pool.wait_ge(gat_hi_ready, NC * g + c + 1)
                pool.tensor_tensor(gat_lo[:, c, :], gw[:], gat_hi[:, c, :].bitcast(F32), ALU.subtract).then_inc(gat_lo_ready, 1)

            def step(g, p, attn, more):
                a = g + 1
                for u in range(NU):
                    k, even = u // 2, u % 2 == 0
                    if even:
                        if 1 <= k <= NC:
                            split_gated(g, k - 1)
                        if attn and 1 <= k <= NB:
                            rstd_x1(a, k - 1)
                        if more and k == NB + 1:
                            mask_bias(a + 1)
                    else:
                        if attn and k < NB:
                            split_ctx(a, k)
                        if attn and k < NB - 2:
                            rstd_x(a, k + 2)
                        if more and k >= NB:
                            rstd_x(a + 1, k - NB)

            def first():
                rstd_x(0, 0)
                rstd_x(0, 1)
                mask_bias(0)
                for k in range(NB + 1):
                    if k < NB - 2:
                        rstd_x(0, k + 2)
                    if 1 <= k <= NB:
                        rstd_x1(0, k - 1)
                    if k < NB:
                        split_ctx(0, k)
                rstd_x(1, 0)
                mask_bias(1)
                rstd_x(1, 1)

            pool.memset(nhalf[:], -0.5).then_inc(set_up, 1)
            pool.wait_ge(set_up, 1)
            first()
            steps(pool, step)


def kernel(x, ctx_2048, mask_BxS2_bk0, L0_ffn_G, L0_ffn_gate_w, L0_ffn_up_w, L0_ffn_down_w, L0_ffn_lora_A, L0_ffn_lora_B):
    import concourse.bacc as bacc
    from concourse.bass_utils import run_bass_kernel_spmd

    def by_chunk(w):
        return w.reshape(KD, P, -1).transpose(1, 0, 2)

    x, ctx = np.asarray(x), np.asarray(ctx_2048)
    ctxT = ctx.transpose(0, 2, 1).reshape(B, KD, P, S).transpose(0, 2, 1, 3)
    mask = np.asarray(mask_BxS2_bk0).reshape(NG, NB, S)
    gate, up = (by_chunk(np.asarray(w).reshape(E * FE, D).T) for w in (L0_ffn_gate_w, L0_ffn_up_w))
    wgu = np.concatenate([gate, up], 2)
    ga = np.concatenate([by_chunk(np.asarray(L0_ffn_G)), by_chunk(np.asarray(L0_ffn_lora_A).reshape(LR, D).T)], 2)
    dn = np.concatenate([by_chunk(np.asarray(L0_ffn_down_w).transpose(0, 2, 1).reshape(E * FE, D)),
                         np.asarray(L0_ffn_lora_B).transpose(0, 2, 1).reshape(P, 1, D)], 1)
    sel = np.zeros((P, NC * P), np.float32)
    for e in range(E):
        sel[e, e * FE:(e + 1) * FE] = sel[E + e, e * FE:(e + 1) * FE] = 1
    earlier = np.tile(np.tril(np.ones((E, E), np.float32), -1).reshape(1, -1), (P, NB))
    consts = np.concatenate([sel, np.eye(P, dtype=np.float32), earlier], 1)

    arrays = {"x": x, "ctx": ctx, "ctxT": ctxT, "mask": mask, "wgu": wgu, "ga": ga, "dn": dn, "consts": consts}
    arrays = {f"in_{n}": np.ascontiguousarray(a) for n, a in arrays.items()}
    nc = bacc.Bacc("TRN2", target_bir_lowering=False, num_devices=1)
    args = [nc.dram_tensor(n, a.shape, mybir.dt.from_np(a.dtype), kind="ExternalInput").ap() for n, a in arrays.items()]
    args.append(nc.dram_tensor("out_x", (B, S, D), F32, kind="ExternalOutput").ap())
    xattn_moe(nc, *args)
    return run_bass_kernel_spmd(nc, [arrays], core_ids=[0]).results[0]["out_x"]
```

```python
from contextlib import ExitStack

import numpy as np
import concourse.bass as bass
from concourse import mybir

F32 = mybir.dt.float32
F32R = mybir.dt.float32r
U8 = mybir.dt.uint8
ALU = mybir.AluOpType
ACT = mybir.ActivationFunctionType
AX = mybir.AxisListType

B, S, D = 64, 128, 512
P = 128
KD = D // P
E, FE, R = 8, 64, 16
NB = 4
NG = B // NB
T = NB * S
NC = E * FE // P
NU = 2 * NC + NB
LR = E * R
GA = E + LR
EPS = 1e-5
BIG = 1e30
RING = 3
H2_AT, READ_AT, ROUTE_AT, SCORES_AT = 1, 3, 3, 1


def past(count, least):
    return not isinstance(count, int) or count >= least


def xattn_moe(nc, x, xT, ctx, ctxT, mask, wgu, ga, dn, consts, out):
    with ExitStack() as stack:
        def sb(name, shape, dt=F32):
            return stack.enter_context(nc.sbuf_tensor(name, [P] + shape, dt))

        def sem(name):
            return stack.enter_context(nc.semaphore(name))

        def bank(name):
            return stack.enter_context(nc.psum_tensor(name, [P, 512], F32))
        ffn_ps = [bank(f"ffn_ps{i}") for i in range(RING)]
        w_ps = bank("w_ps")
        mean_ps = bank("mean_ps")
        sr_ps = bank("sr_ps")
        pv_ps = bank("pv_ps")
        h2T_ps = bank("h2T_ps")

        wgu_hi, wgu_lo = sb("wgu_hi", [KD, 2 * E * FE], F32R), sb("wgu_lo", [KD, 2 * E * FE], F32R)
        ga_raw = sb("ga_raw", [KD, GA])
        ga_r = sb("ga_r", [KD, 2 * GA], F32R)
        dn_raw = sb("dn_raw", [NC + 1, D])
        dn_hi, dn_lo = sb("dn_hi", [NC + 1, D], F32R), sb("dn_lo", [NC + 1, D], F32R)
        const_sb = sb("const_sb", [P + NC * P + NB * E * E])
        sel = sb("sel", [NC, P], F32R)
        ident = const_sb[:, 0:P]
        earlier = const_sb[:, P + NC * P:].rearrange("p (b e f) -> p b e f", b=NB, e=E)
        ident_r = sb("ident_r", [P], F32R)
        nhalf = sb("nhalf", [1])

        x_sb = sb("x_sb", [NB, D])
        xT_sb = sb("xT_sb", [NB, KD, P])
        ctx_sb = sb("ctx_sb", [NB, D])
        ctxT_sb = sb("ctxT_sb", [NB, KD, P])
        mask_sb = sb("mask_sb", [NB, S], U8)
        bias = sb("bias", [NB, S])
        valid, offset = sb("valid", [NB]), sb("offset", [NB])
        masked = sb("masked", [S])
        rowmax, negmax = sb("rowmax", [1]), sb("negmax", [1])
        prob, rowsum = sb("prob", [S]), sb("rowsum", [1])
        rinv, rinv_v = sb("rinv", [1]), sb("rinv_v", [1])
        pT_hi, pT_lo = sb("pT_hi", [S], F32R), sb("pT_lo", [S], F32R)
        ctx_hi, ctx_lo = sb("ctx_hi", [D], F32R), sb("ctx_lo", [D], F32R)
        x1 = sb("x1", [2, NB, D])
        h2 = sb("h2", [D])
        st1, mv1 = sb("st1", [6]), sb("mv1", [NB, 2])
        var1, scale1 = sb("var1", [NB]), sb("scale1", [NB])
        st2, mv2, ln2 = sb("st2", [6]), sb("mv2", [2]), sb("ln2", [3])

        h2T_hi, h2T_lo = sb("h2T_hi", [2, KD, T], F32R), sb("h2T_lo", [2, KD, T], F32R)
        router = sb("router", [NB, GA])
        lmax, lexp, lsum, linv = sb("lmax", [NB]), sb("lexp", [NB, E]), sb("lsum", [NB]), sb("linv", [NB])
        gt, eq = sb("gt", [NB, E, E]), sb("eq", [NB, E, E])
        rank, rw = sb("rank", [NB, E]), sb("rw", [NB, E])
        whi = sb("whi", [NB, E], F32R)
        wpad = sb("wpad", [NB, P], F32R)
        lrw = sb("lrw", [NB, LR])
        wT = sb("wT", [T], F32R)
        work = sb("work", [4, T])
        th, t1, gw = work[:, 0, :], work[:, 1, :], work[:, 2, :]
        gat_hi, gat_lo = sb("gat_hi", [NC + 1, T], F32R), sb("gat_lo", [NC + 1, T], F32R)

        wgu_loaded = [sem(f"wgu_loaded{k}") for k in range(KD)]
        ga_loaded, dn_loaded, ident_loaded, const_loaded = map(sem, ("ga_loaded", "dn_loaded", "ident_loaded", "const_loaded"))
        x_loaded = [sem(f"x_loaded{b}") for b in range(NB)]
        xT_loaded = [sem(f"xT_loaded{b}") for b in range(NB)]
        ctx_loaded = [sem(f"ctx_loaded{b}") for b in range(NB)]
        ctxT_loaded = [sem(f"ctxT_loaded{b}") for b in range(NB)]
        mask_loaded = sem("mask_loaded")
        stored = [sem(f"stored{b}") for b in range(NB)]
        w_hi_ready, w_ready = sem("w_hi_ready"), sem("w_ready")
        ga_ready, sel_ready = sem("ga_ready"), sem("sel_ready")
        set_up = sem("set_up")
        bias_ready, valid_ready = sem("bias_ready"), sem("valid_ready")
        st1_done, mv1_ready, scale1_step = map(sem, ("st1_done", "mv1_ready", "scale1_step"))
        st2_done, mv2_ready, ln2_step, h2_ready = map(sem, ("st2_done", "mv2_ready", "ln2_step", "h2_ready"))
        mean_done, centred = sem("mean_done"), sem("centred")
        scores_done, masked_ready, negmax_ready, prob_ready = map(sem, ("scores_done", "masked_ready", "negmax_ready", "prob_ready"))
        rinv_step, pT_done, pT_hi_ready, pT_lo_ready = map(sem, ("rinv_step", "pT_done", "pT_hi_ready", "pT_lo_ready"))
        ctx_hi_ready, ctx_lo_ready = sem("ctx_hi_ready"), sem("ctx_lo_ready")
        pv_done, x1_ready = sem("pv_done"), sem("x1_ready")
        h2T_done, h2T_hi_ready, h2T_lo_ready = map(sem, ("h2T_done", "h2T_hi_ready", "h2T_lo_ready"))
        router_done, lr_ready = sem("router_done"), sem("lr_ready")
        rt, lexp_ready, rw_ready = sem("rt"), sem("lexp_ready"), sem("rw_ready")
        wT_done, wT_ready = sem("wT_done"), sem("wT_ready")
        lrT_done, lr_hi_ready, lr_lo_ready = map(sem, ("lrT_done", "lr_hi_ready", "lr_lo_ready"))
        gate_up_done = sem("gate_up_done")
        th_ready, t1_ready, t2_ready, wb_done, gw_ready, gat_hi_ready, gat_lo_ready = map(
            sem, ("th_ready", "t1_ready", "t2_ready", "wb_done", "gw_ready", "gat_hi_ready", "gat_lo_ready"))
        down_done, out_ready = sem("down_done"), sem("out_ready")
        sp_waited, dve_waited, pool_waited = sem("sp_waited"), sem("dve_waited"), sem("pool_waited")
        RT = 13
        LEAD = 1

        def wgu_part(k):
            place = work[:] if k < KD // 2 else x1[:, 1, :, :]
            return place.rearrange("p c t -> p (c t)")[:, k % (KD // 2) * 2 * E * FE:(k % (KD // 2) + 1) * 2 * E * FE]

        block = stack.enter_context(nc.Block())

        def steps(engine, step):
            step(0, 0, True, True)
            with engine.Fori(0, (NG - 4) // 2) as i:
                step(2 * i + 1, 1, True, True)
                step(2 * i + 2, 0, True, True)
            step(NG - 3, 1, True, True)
            step(NG - 2, 0, True, False)
            step(NG - 1, 1, False, False)

        @block.sync
        def _(sp):
            def load_x(g, b):
                sp.dma_start(x_sb[:, b, :], x[NB * g + b]).then_inc(x_loaded[b], 16)

            def load_xT(g, b):
                sp.dma_start(xT_sb[:, b, :, :], xT[NB * g + b]).then_inc(xT_loaded[b], 16)

            def load_ctx(g, b):
                sp.dma_start(ctxT_sb[:, b, :, :], ctxT[NB * g + b]).then_inc(ctxT_loaded[b], 16)
                sp.dma_start(ctx_sb[:, b, :], ctx[NB * g + b]).then_inc(ctx_loaded[b], 16)

            def load_mask(g):
                sp.dma_start(mask_sb[:], mask[g].partition_broadcast(P)).then_inc(mask_loaded, 16)

            def load_weights(k):
                sp.dma_start(wgu_part(k), wgu[:, k, :]).then_inc(wgu_loaded[k], 16)

            load_mask(0)
            load_x(0, 0)
            sp.dma_start(const_sb[:, 0:P], consts[:, 0:P]).then_inc(ident_loaded, 16)
            load_xT(0, 0)
            load_ctx(0, 0)
            load_x(0, 1)
            load_xT(0, 1)
            load_x(0, 2)
            load_x(0, 3)
            sp.dma_start(ga_raw[:], ga).then_inc(ga_loaded, 16)
            load_ctx(0, 1)
            load_weights(0)
            load_xT(0, 2)
            load_ctx(0, 2)
            load_weights(1)
            load_xT(0, 3)
            load_ctx(0, 3)
            sp.dma_start(const_sb[:, P:], consts[:, P:]).then_inc(const_loaded, 16)
            load_weights(2)
            load_weights(3)
            sp.dma_start(dn_raw[:], dn).then_inc(dn_loaded, 16)

            def step(g, p, attn, more):
                a = g + 1
                if more:
                    sp.wait_ge(bias_ready, a + 1)
                    sp.wait_ge(valid_ready, 2 * a + 2)
                    sp.sem_inc(sp_waited, 1)
                    load_mask(a + 1)
                    for b in range(NB):
                        n = NB * a + b
                        sp.wait_ge(x1_ready, n + 1)
                        sp.wait_ge(scores_done, n + 1)
                        sp.wait_ge(ctx_lo_ready, n + 1)
                        sp.sem_inc(sp_waited, 1)
                        load_x(a + 1, b)
                        load_xT(a + 1, b)
                        load_ctx(a + 1, b)
                if past(g, 0):
                    for b in range(NB):
                        sp.wait_ge(out_ready, NB * g + b + 1)
                        sp.sem_inc(sp_waited, 1)
                        sp.dma_start(out[NB * g + b], x1[:, p, b, :]).then_inc(stored[b], 16)

            step(-1, 1, True, True)
            steps(sp, step)
            for b in range(NB):
                sp.wait_ge(stored[b], 16 * NG)

        @block.tensor
        def _(pe):
            def three(psum, hi, lo, x_hi, x_lo, start, stop):
                pe.matmul(psum, hi, x_hi, start=start, stop=False)
                pe.matmul(psum, hi, x_lo, start=False, stop=False)
                return pe.matmul(psum, lo, x_hi, start=False, stop=stop)

            def turn_mean(a, b):
                n = NB * a + b
                pe.wait_ge(mv1_ready, n + 1)
                if past(n, 1):
                    pe.wait_ge(centred, n)
                pe.transpose(mean_ps[:, 0:P], mv1[:, b, 0:1].broadcast_to([P, P]), ident).then_inc(mean_done, 1)

            def scores(a, b):
                n = NB * a + b
                pe.wait_ge(centred, n + 1)
                pe.wait_ge(ctxT_loaded[b], 16 * (a + 1))
                if past(n, 1):
                    pe.wait_ge(masked_ready, n)
                if past(a, 1) and (b == 0 or b > LEAD):
                    pe.wait_ge(lr_ready, n if b == 0 else n - LEAD)
                for k in range(KD):
                    mm = pe.matmul(sr_ps[:, 0:S], xT_sb[:, b, k, :], ctxT_sb[:, b, k, :], start=(k == 0), stop=(k == KD - 1))
                mm.then_inc(scores_done, 1)

            def turn_prob(a, b):
                n = NB * a + b
                pe.wait_ge(prob_ready, n + 1)
                if past(n, 1):
                    pe.wait_ge(x1_ready, n)
                pe.transpose(pv_ps[:, 0:S], prob[:], ident).then_inc(pT_done, 1)

            def readout(a, b):
                n = NB * a + b
                pe.wait_ge(pT_lo_ready, n + 1)
                pe.wait_ge(ctx_lo_ready, n + 1)
                three(pv_ps[:], pT_hi[:], pT_lo[:], ctx_hi[:], ctx_lo[:], True, True).then_inc(pv_done, 1)

            def turn_h2(a, b):
                n = NB * a + b
                pe.wait_ge(h2_ready, n + 1)
                if past(n, 1):
                    pe.wait_ge(h2T_lo_ready, n)
                if b == 0 and past(a, 1):
                    pe.wait_ge(lr_lo_ready, a)
                for k in range(KD):
                    mm = pe.transpose(h2T_ps[:, k * P:(k + 1) * P], h2[:, k * P:(k + 1) * P], ident)
                mm.then_inc(h2T_done, 1)

            def route(a, q, b, ps=sr_ps):
                n = NB * a + b
                if b == 0 and not past(n, 1):
                    pe.wait_ge(ga_ready, 1)
                pe.wait_ge(h2T_lo_ready, n + 1)
                if past(a, 1):
                    pe.wait_ge(masked_ready, n + 1 + min(LEAD, NB - 1 - b))
                elif b:
                    pe.wait_ge(lr_ready, b)
                for k in range(KD):
                    pe.matmul(ps[:, 0:2 * GA], h2T_hi[:, q, k, b * S:(b + 1) * S], ga_r[:, k, :], start=(k == 0), stop=False)
                    mm = pe.matmul(ps[:, 0:2 * GA], h2T_lo[:, q, k, b * S:(b + 1) * S], ga_r[:, k, :], start=False, stop=(k == KD - 1))
                mm.then_inc(router_done, 1)

            def turn_weights(g):
                pe.wait_ge(rw_ready, g + 1)
                if past(g, 1):
                    pe.wait_ge(gw_ready, NC * g)
                for b in range(NB):
                    mm = pe.transpose(w_ps[:, b * S:(b + 1) * S].bitcast(F32R), wpad[:, b, :], ident_r[:])
                mm.then_inc(wT_done, 1)
                pe.wait_ge(h2T_lo_ready, NB * g + NB)
                for b in range(NB):
                    mm = pe.transpose(h2T_ps[:, b * S:(b + 1) * S], lrw[:, b, :], ident)
                mm.then_inc(lrT_done, 1)

            def spread(g, c):
                if c == 0:
                    pe.wait_ge(wT_ready, g + 1)
                    if not past(g, 1):
                        pe.wait_ge(sel_ready, 1)
                else:
                    pe.wait_ge(gw_ready, NC * g + c)
                pe.matmul(w_ps[:], sel[:, c, :], wT[:], start=True, stop=True).then_inc(wb_done, 1)

            def ffn_unit(g, p, u, between):
                ps = ffn_ps[u % RING]
                v = u - RING
                if v < 0:
                    if past(g, 1):
                        pe.wait_ge(out_ready, NB * g + v + 1)
                    elif u == 2:
                        pe.wait_ge(lr_ready, NB)
                elif v >= 2 * NC:
                    pe.wait_ge(out_ready, NB * g + v - 2 * NC + 1)
                elif v % 2 == 0:
                    pe.wait_ge(t1_ready, NC * g + v // 2 + 1)
                else:
                    pe.wait_ge(t2_ready, NC * g + v // 2 + 1)
                if u < 2 * NC:
                    c, col = u // 2, (u % 2) * E * FE + (u // 2) * P
                    if u == 0:
                        pe.wait_ge(h2T_lo_ready, NB * g + NB)
                        if not past(g, 1):
                            pe.wait_ge(w_ready, KD)
                    for k in range(KD):
                        between(k)
                        mm = three(ps[:], wgu_hi[:, k, col:col + P], wgu_lo[:, k, col:col + P],
                                   h2T_hi[:, p, k, :], h2T_lo[:, p, k, :], k == 0, k == KD - 1)
                    mm.then_inc(gate_up_done, 1)
                else:
                    b = u - 2 * NC
                    if b == 0:
                        if not past(g, 1):
                            pe.wait_ge(w_ready, KD + 1)
                        pe.wait_ge(lr_lo_ready, g + 1)
                    order = [NC] + list(range(NC))
                    for j, c in enumerate(order):
                        between(j)
                        if b == 0 and c < NC:
                            pe.wait_ge(gat_lo_ready, NC * g + c + 1)
                        tok = slice(b * S, (b + 1) * S)
                        hi, lo, w_hi, w_lo = gat_hi[:, c, tok], gat_lo[:, c, tok], dn_hi[:, c, :], dn_lo[:, c, :]
                        mm = three(ps[:], hi, lo, w_hi, w_lo, j == 0, j == NC)
                    mm.then_inc(down_done, 1)

            def step(g, p, attn, more):
                a, q = g + 1, 1 - p
                for u in range(NU):
                    k, even = u // 2, u % 2 == 0
                    if attn and even and 1 <= k <= NB:
                        turn_prob(a, k - 1)

                    def between(done):
                        if attn and even and done == H2_AT and 2 <= k < NB + 2:
                            turn_h2(a, k - 2)
                        if attn and even and done == READ_AT and 1 <= k <= NB:
                            readout(a, k - 1)
                        if attn and even and done == ROUTE_AT and 2 <= k < NB + 2:
                            route(a, q, k - 2)
                        if attn and not even and done == SCORES_AT and k < NB:
                            scores(a, k)
                        if attn and not even and done == SCORES_AT and k < NB - 1:
                            turn_mean(a, k + 1)
                        if more and not even and done == SCORES_AT and k == NC + 1:
                            turn_mean(a + 1, 0)
                        if not even and done == SCORES_AT and k == 0:
                            turn_weights(g)
                    ffn_unit(g, p, u, between)
                    if u < 2 * NC:
                        between(KD)
                    if not even and k < NC:
                        spread(g, k)

            def first():
                turn_mean(0, 0)
                for k in range(NB + 3):
                    if 1 <= k <= NB:
                        turn_prob(0, k - 1)
                    if k < NB:
                        scores(0, k)
                    if k < NB - 1:
                        turn_mean(0, k + 1)
                    if 1 <= k <= NB:
                        readout(0, k - 1)
                    if k >= 3:
                        route(0, 0, k - 3, ffn_ps[2])
                    if 2 <= k < NB + 2:
                        turn_h2(0, k - 2)
                turn_mean(1, 0)

            pe.wait_ge(ident_loaded, 16)
            first()
            steps(pe, step)

        @block.scalar
        def _(act):
            def keep_h2T(a, g, q, b):
                n = NB * a + b
                act.wait_ge(h2T_done, n + 1)
                if b == 0 and past(g, 1):
                    act.wait_ge(gate_up_done, 2 * NC * g)
                act.copy(h2T_hi[:, q, :, b * S:(b + 1) * S], h2T_ps[:].rearrange("p (k s) -> p k s", k=KD)).then_inc(h2T_hi_ready, 1)

            def keep_pT(a, b):
                n = NB * a + b
                act.wait_ge(pT_done, n + 1)
                if past(n, 1):
                    act.wait_ge(pv_done, n)
                act.copy(pT_hi[:], pv_ps[:, 0:S]).then_inc(pT_hi_ready, 1)

            def split_gated(g, c):
                act.wait_ge(gw_ready, NC * g + c + 1)
                if c == 0 and past(g, 1):
                    act.wait_ge(down_done, NB * g)
                act.copy(gat_hi[:, c, :], gw).then_inc(gat_hi_ready, 1)

            def half_tanh(g, c):
                act.wait_ge(gate_up_done, 2 * NC * g + 2 * c + 1)
                if c or past(g, 1):
                    act.wait_ge(t1_ready, NC * g + c)
                act.activation(th, ffn_ps[2 * c % RING][:], ACT.Tanh, scale=0.5).then_inc(th_ready, 1)

            def keep_weights(g):
                act.wait_ge(wT_done, g + 1)
                if past(g, 1):
                    act.wait_ge(wb_done, NC * g)
                act.copy(wT[:], w_ps[:]).then_inc(wT_ready, 1)

            def keep_lrT(g):
                act.wait_ge(lrT_done, g + 1)
                if past(g, 1):
                    act.wait_ge(down_done, NB * g)
                act.copy(gat_hi[:, NC, :], h2T_ps[:]).then_inc(lr_hi_ready, 1)

            def softmax_exp(a, b):
                n = NB * a + b
                act.wait_ge(negmax_ready, n + 1)
                if past(n, 1):
                    act.wait_ge(pT_done, n)
                    act.wait_ge(rinv_step, 2 * n)
                act.activation(prob[:], masked[:], ACT.Exp, scale=scale1[:, b:b + 1], bias=negmax[:], accum_out=rowsum[:]).then_inc(prob_ready, 1)

            def split_ctx(a, b):
                n = NB * a + b
                act.wait_ge(ctx_loaded[b], 16 * (a + 1))
                if past(n, 1):
                    act.wait_ge(pv_done, n)
                act.copy(ctx_hi[:], ctx_sb[:, b, :]).then_inc(ctx_hi_ready, 1)

            def normalise_x1(a, b, p):
                n = NB * a + b
                act.wait_ge(ln2_step, 3 * n + 3)
                if past(n, 1):
                    act.wait_ge(h2T_done, n)
                act.activation(h2[:], x1[:, 1 - p, b, :], ACT.Identity, scale=ln2[:, 1:2], bias=ln2[:, 2:3]).then_inc(h2_ready, 1)

            def mask_bias(a):
                act.wait_ge(valid_ready, 2 * a + 2)
                if past(a, 1):
                    act.wait_ge(masked_ready, NB * a)
                for b in range(NB):
                    copy = act.activation(bias[:, b, :], mask_sb[:, b, :], ACT.Identity, scale=BIG, bias=offset[:, b:b + 1])
                copy.then_inc(bias_ready, 1)

            def router_exp(a):
                act.wait_ge(rt, RT * a + 2)
                act.activation(lexp[:], lexp[:], ACT.Exp).then_inc(lexp_ready, 1)

            def step(g, p, attn, more):
                a, q = g + 1, 1 - p
                for u in range(NU):
                    k, even = u // 2, u % 2 == 0
                    if even:
                        if attn and 1 <= k <= NB:
                            keep_pT(a, k - 1)
                        if attn and 2 <= k < NB + 2:
                            keep_h2T(a, g, q, k - 2)
                        if 1 <= k <= NC:
                            split_gated(g, k - 1)
                        if k < NC:
                            half_tanh(g, k)
                        if attn and k == NB + 1:
                            router_exp(a)
                        if more and k == NB + 1:
                            mask_bias(a + 1)
                    else:
                        if attn and k < NB:
                            split_ctx(a, k)
                            softmax_exp(a, k)
                        if k == 0:
                            keep_weights(g)
                            keep_lrT(g)
                        if attn and 1 <= k <= NB:
                            normalise_x1(a, k - 1, p)

            def weights_hi(k):
                if k == 0:
                    act.wait_ge(ga_loaded, 16)
                    act.copy(ga_r[:, :, 0:GA], ga_raw[:]).then_inc(w_hi_ready, 1)
                elif k <= KD:
                    act.wait_ge(wgu_loaded[k - 1], 16)
                    act.copy(wgu_hi[:, k - 1, :], wgu_part(k - 1)).then_inc(w_hi_ready, 1)
                else:
                    act.wait_ge(dn_loaded, 16)
                    act.copy(dn_hi[:], dn_raw[:]).then_inc(w_hi_ready, 1)

            def first():
                mask_bias(0)
                for k in range(NB + 2):
                    if 1 <= k <= NB:
                        keep_pT(0, k - 1)
                    if k >= 2:
                        normalise_x1(0, k - 2, 1)
                    if k < NB:
                        softmax_exp(0, k)
                    if k >= 2:
                        keep_h2T(0, -1, 0, k - 2)
                    if k < NB:
                        split_ctx(0, k)
                    weights_hi(k)
                router_exp(0)
                mask_bias(1)

            first()
            steps(act, step)

        @block.vector
        def _(dve):
            def stats_x(a, b):
                n = NB * a + b
                dve.wait_ge(x_loaded[b], 16 * (a + 1))
                if past(n, 1):
                    dve.wait_ge(mv1_ready, n)
                dve.bn_stats(st1[:], x_sb[:, b, :]).then_inc(st1_done, 1)
                dve.wait_ge(st1_done, n + 1)
                if past(a, 1):
                    dve.wait_ge(scale1_step, 2 * (n - NB) + 1)
                    dve.wait_ge(mean_done, n - NB + 1)
                dve.sem_inc(dve_waited, 1)
                dve.bn_aggr(mv1[:, b, :], st1[:]).then_inc(mv1_ready, 1)

            def centre(a, b):
                n = NB * a + b
                dve.wait_ge(mean_done, n + 1)
                dve.wait_ge(xT_loaded[b], 16 * (a + 1))
                dve.tensor_tensor(xT_sb[:, b, :, :], xT_sb[:, b, :, :],
                                  mean_ps[:, 0:P].rearrange("p (o s) -> p o s", o=1).broadcast_to([P, KD, P]),
                                  ALU.subtract).then_inc(centred, 1)

            def stats_x1(a, b, q):
                n = NB * a + b
                dve.wait_ge(x1_ready, n + 1)
                if past(n, 1):
                    dve.wait_ge(mv2_ready, n)
                dve.bn_stats(st2[:], x1[:, q, b, :]).then_inc(st2_done, 1)
                dve.wait_ge(st2_done, n + 1)
                if past(n, 1):
                    dve.wait_ge(ln2_step, 3 * n)
                dve.sem_inc(dve_waited, 1)
                dve.bn_aggr(mv2[:], st2[:]).then_inc(mv2_ready, 1)

            def any_valid(a):
                dve.wait_ge(mask_loaded, 16 * (a + 1))
                if past(a, 1):
                    dve.wait_ge(rinv_step, 2 * NB * a)
                    dve.wait_ge(bias_ready, a)
                dve.tensor_reduce(valid[:], mask_sb[:], AX.X, ALU.max).then_inc(valid_ready, 1)
                dve.wait_ge(valid_ready, 2 * a + 1)
                dve.tensor_scalar(offset[:], valid[:], -BIG, None, ALU.mult).then_inc(valid_ready, 1)

            def split_pT(a, b):
                n = NB * a + b
                dve.wait_ge(pT_hi_ready, n + 1)
                dve.tensor_tensor(pT_lo[:], pv_ps[:, 0:S], pT_hi[:].bitcast(F32), ALU.subtract).then_inc(pT_lo_ready, 1)

            def split_h2T(a, q, b):
                n = NB * a + b
                dve.wait_ge(h2T_hi_ready, n + 1)
                dve.tensor_tensor(h2T_lo[:, q, :, b * S:(b + 1) * S], h2T_ps[:].rearrange("p (k s) -> p k s", k=KD),
                                  h2T_hi[:, q, :, b * S:(b + 1) * S].bitcast(F32), ALU.subtract).then_inc(h2T_lo_ready, 1)

            def times_up(g, c):
                m = NC * g + c
                dve.wait_ge(gate_up_done, 2 * NC * g + 2 * c + 2)
                dve.wait_ge(t1_ready, m + 1)
                dve.tensor_tensor(t1, t1, ffn_ps[(2 * c + 1) % RING][:], ALU.mult).then_inc(t2_ready, 1)

            def times_weight(g, c):
                m = NC * g + c
                dve.wait_ge(wb_done, m + 1)
                dve.wait_ge(t2_ready, m + 1)
                if c or past(g, 1):
                    dve.wait_ge(gat_lo_ready, m)
                dve.tensor_tensor(gw, t1, w_ps[:], ALU.mult).then_inc(gw_ready, 1)

            def router_sums(a, b, ps=sr_ps):
                n = NB * a + b
                dve.wait_ge(router_done, n + 1)
                dve.tensor_reduce(router[:, b, :], ps[:, 0:2 * GA].rearrange("p (part f) -> p f part", part=2),
                                  AX.X, ALU.add).then_inc(lr_ready, 1)

            def gate_times_up(g, c):
                dve.wait_ge(th_ready, NC * g + c + 1)
                dve.scalar_tensor_tensor(out=t1, in0=th, scalar=1.0, in1=ffn_ps[2 * c % RING][:],
                                         op0=ALU.add, op1=ALU.mult).then_inc(t1_ready, 1)

            def row_weights(a, b):
                n = NB * a + b
                dve.wait_ge(prob_ready, n + 1)
                if past(n, 1):
                    dve.wait_ge(x1_ready, n)
                dve.reciprocal(rinv[:], rowsum[:]).then_inc(rinv_step, 1)
                dve.wait_ge(rinv_step, 2 * n + 1)
                if b == 0:
                    dve.wait_ge(valid_ready, 2 * a + 2)
                dve.tensor_tensor(rinv_v[:], rinv[:], valid[:, b:b + 1], ALU.mult).then_inc(rinv_step, 1)

            def add_readout(a, q, b):
                n = NB * a + b
                dve.wait_ge(rinv_step, 2 * n + 2)
                dve.wait_ge(pv_done, n + 1)
                if b == 0 and q == 1 and not past(a, 2):
                    dve.wait_ge(w_ready, KD)
                if past(a, 2):
                    dve.wait_ge(stored[b], 16 * (a - 1))
                dve.scalar_tensor_tensor(out=x1[:, q, b, :], in0=pv_ps[:], scalar=rinv_v[:], in1=x_sb[:, b, :],
                                         op0=ALU.mult, op1=ALU.add).then_inc(x1_ready, 1)

            def mask_scores(a, b):
                n = NB * a + b
                dve.wait_ge(scores_done, n + 1)
                if b == 0:
                    dve.wait_ge(bias_ready, a + 1)
                if past(n, 1):
                    dve.wait_ge(prob_ready, n)
                dve.sem_inc(dve_waited, 1)
                dve.tensor_tensor_reduce(masked[:], sr_ps[:, 0:S], bias[:, b, :], 1.0, -3e38, ALU.add, ALU.max,
                                         rowmax[:]).then_inc(masked_ready, 1)
                dve.wait_ge(masked_ready, n + 1)
                dve.wait_ge(scale1_step, 2 * n + 2)
                dve.tensor_scalar(negmax[:], rowmax[:], scale1[:, b:b + 1], -1.0, ALU.mult, ALU.mult).then_inc(negmax_ready, 1)

            def add_ffn(g, p, b):
                dve.wait_ge(down_done, NB * g + b + 1)
                dve.tensor_tensor(x1[:, p, b, :], ffn_ps[(2 * NC + b) % RING][:], x1[:, p, b, :], ALU.add).then_inc(out_ready, 1)

            def split_lr(g):
                dve.wait_ge(lr_hi_ready, g + 1)
                dve.tensor_tensor(gat_lo[:, NC, :], h2T_ps[:], gat_hi[:, NC, :].bitcast(F32), ALU.subtract).then_inc(lr_lo_ready, 1)

            def route(a):
                def over(v):
                    return v.rearrange("p (b o) -> p b o", o=1).broadcast_to([P, NB, E])
                s = RT * a
                logits, lr = router[:, :, 0:E], router[:, :, E:]
                dve.wait_ge(lr_ready, NB * a + NB)
                dve.tensor_reduce(lmax[:], logits, AX.X, ALU.max).then_inc(rt, 1)
                dve.wait_ge(rt, s + 1)
                dve.tensor_tensor(lexp[:], logits, over(lmax[:]), ALU.subtract).then_inc(rt, 1)
                dve.wait_ge(lexp_ready, a + 1)
                dve.tensor_reduce(lsum[:], lexp[:], AX.X, ALU.add).then_inc(rt, 1)
                dve.wait_ge(rt, s + 3)
                dve.reciprocal(linv[:], lsum[:]).then_inc(rt, 1)
                dve.wait_ge(rt, s + 4)
                dve.tensor_tensor(lexp[:], lexp[:], over(linv[:]), ALU.mult).then_inc(rt, 1)
                dve.wait_ge(rt, s + 5)
                own = lexp[:].rearrange("p b (e o) -> p b e o", o=1).broadcast_to([P, NB, E, E])
                other = lexp[:].rearrange("p b (o e) -> p b o e", o=1).broadcast_to([P, NB, E, E])
                dve.tensor_tensor(gt[:], other, own, ALU.is_gt).then_inc(rt, 1)
                dve.tensor_tensor(eq[:], other, own, ALU.is_equal).then_inc(rt, 1)
                dve.wait_ge(rt, s + 7)
                dve.tensor_tensor(eq[:], eq[:], earlier, ALU.mult).then_inc(rt, 1)
                dve.wait_ge(rt, s + 8)
                dve.tensor_tensor(gt[:], gt[:], eq[:], ALU.add).then_inc(rt, 1)
                dve.wait_ge(rt, s + 9)
                dve.tensor_reduce(rank[:], gt[:], AX.X, ALU.add).then_inc(rt, 1)
                dve.wait_ge(rt, s + 10)
                dve.scalar_tensor_tensor(out=rw[:], in0=rank[:], scalar=1.5, in1=lexp[:], op0=ALU.is_lt, op1=ALU.mult).then_inc(rt, 1)
                dve.wait_ge(rt, s + 11)
                if past(a, 1):
                    dve.wait_ge(lrT_done, a)
                dve.tensor_scalar(whi[:], rw[:], 0.5, None, ALU.mult).then_inc(rt, 1)
                dve.wait_ge(rt, s + 12)
                dve.tensor_copy(wpad[:, :, 0:E], whi[:]).then_inc(rt, 1)
                dve.scalar_tensor_tensor(out=wpad[:, :, E:2 * E], in0=rw[:], scalar=0.5, in1=whi[:].bitcast(F32),
                                         op0=ALU.mult, op1=ALU.subtract)
                dve.tensor_tensor(lrw[:].rearrange("p b (e r) -> p b e r", e=E), lr.rearrange("p b (e r) -> p b e r", e=E),
                                  rw[:].rearrange("p b (e o) -> p b e o", o=1).broadcast_to([P, NB, E, R]),
                                  ALU.mult).then_inc(rw_ready, 1)

            def step(g, p, attn, more):
                a, q = g + 1, 1 - p
                for u in range(NU):
                    k, even = u // 2, u % 2 == 0
                    if even:
                        if attn and k == 0:
                            stats_x(a, 2)
                        if 1 <= k <= NC:
                            times_up(g, k - 1)
                        if attn and 1 <= k <= NB:
                            split_pT(a, k - 1)
                        if 1 <= k <= NC:
                            times_weight(g, k - 1)
                        if attn and 1 <= k <= NB:
                            row_weights(a, k - 1)
                        if attn and 2 <= k < NB + 2:
                            split_h2T(a, q, k - 2)
                        if k == NC + 1:
                            add_ffn(g, p, 1)
                        if more and k == NB + 1:
                            stats_x(a + 1, 1)
                        if attn and 1 <= k <= NB:
                            add_readout(a, q, k - 1)
                        if attn and 2 <= k < NB + 2:
                            router_sums(a, k - 2)
                        if attn and 1 <= k <= NB:
                            stats_x1(a, k - 1, q)
                        if k == 1:
                            split_lr(g)
                    else:
                        if attn and k < NB:
                            mask_scores(a, k)
                        if k < NC:
                            gate_times_up(g, k)
                        if attn and k < NB - 1:
                            centre(a, k + 1)
                        if attn and k == 1:
                            stats_x(a, 3)
                        if k == NC:
                            add_ffn(g, p, 0)
                        if more and k == NB:
                            any_valid(a + 1)
                        if more and k == NB:
                            stats_x(a + 1, 0)
                        if k == NC + 1:
                            add_ffn(g, p, 2)
                        if attn and k == NB + 1:
                            route(a)
                        if more and k == NB + 1:
                            centre(a + 1, 0)
                        if k == NC + 1:
                            add_ffn(g, p, 3)

            def first():
                stats_x(0, 0)
                any_valid(0)
                centre(0, 0)
                for b in range(1, NB):
                    stats_x(0, b)
                dve.memset(wpad[:].bitcast(F32), 0.0)
                for k in range(NB + 3):
                    if 1 <= k <= NB:
                        split_pT(0, k - 1)
                    if k < NB:
                        mask_scores(0, k)
                    if 1 <= k <= NB:
                        row_weights(0, k - 1)
                        add_readout(0, 0, k - 1)
                        stats_x1(0, k - 1, 0)
                    if 2 <= k < NB + 2:
                        split_h2T(0, 0, k - 2)
                    if k < NB - 1:
                        centre(0, k + 1)
                    if k == 1:
                        dve.wait_ge(w_hi_ready, 1)
                        dve.tensor_tensor(ga_r[:, :, GA:], ga_raw[:], ga_r[:, :, 0:GA].bitcast(F32), ALU.subtract).then_inc(ga_ready, 1)
                    if k == 2:
                        dve.wait_ge(const_loaded, 16)
                        dve.tensor_copy(sel[:], const_sb[:, P:P + NC * P].rearrange("p (c f) -> p c f", c=NC)).then_inc(sel_ready, 1)
                        dve.tensor_copy(ident_r[:], ident)
                    if k >= 3:
                        router_sums(0, k - 3, ffn_ps[2])
                    if NB <= k < NB + 2:
                        stats_x(1, k - NB)
                route(0)
                any_valid(1)
                centre(1, 0)

            first()
            steps(dve, step)

        @block.gpsimd
        def _(pool):
            def scale_x(a, b):
                n = NB * a + b
                pool.wait_ge(mv1_ready, n + 1)
                if past(a, 1):
                    pool.wait_ge(prob_ready, n - NB + 1)
                pool.sem_inc(pool_waited, 1)
                pool.tensor_scalar(var1[:, b:b + 1], mv1[:, b, 1:2], float(D), EPS * D, ALU.mult, ALU.add).then_inc(scale1_step, 1)
                pool.wait_ge(scale1_step, 2 * n + 1)
                pool.tensor_tensor(scale1[:, b:b + 1], var1[:, b:b + 1], nhalf[:], ALU.pow).then_inc(scale1_step, 1)

            def rstd_x1(a, b):
                n = NB * a + b
                pool.wait_ge(mv2_ready, n + 1)
                if past(n, 1):
                    pool.wait_ge(h2_ready, n)
                pool.sem_inc(pool_waited, 1)
                pool.tensor_scalar(ln2[:, 0:1], mv2[:, 1:2], EPS, None, ALU.add).then_inc(ln2_step, 1)
                pool.wait_ge(ln2_step, 3 * n + 1)
                pool.tensor_tensor(ln2[:, 1:2], ln2[:, 0:1], nhalf[:], ALU.pow).then_inc(ln2_step, 1)
                pool.wait_ge(ln2_step, 3 * n + 2)
                pool.sem_inc(pool_waited, 1)
                pool.tensor_scalar(ln2[:, 2:3], mv2[:, 0:1], ln2[:, 1:2], -1.0, ALU.mult, ALU.mult).then_inc(ln2_step, 1)

            def split_ctx(a, b):
                n = NB * a + b
                pool.wait_ge(ctx_hi_ready, n + 1)
                pool.tensor_tensor(ctx_lo[:], ctx_sb[:, b, :], ctx_hi[:].bitcast(F32), ALU.subtract).then_inc(ctx_lo_ready, 1)

            def split_gated(g, c):
                pool.wait_ge(gat_hi_ready, NC * g + c + 1)
                pool.tensor_tensor(gat_lo[:, c, :], gw, gat_hi[:, c, :].bitcast(F32), ALU.subtract).then_inc(gat_lo_ready, 1)

            def step(g, p, attn, more):
                a = g + 1
                for u in range(NU):
                    k, even = u // 2, u % 2 == 0
                    if even:
                        if 1 <= k <= NC:
                            split_gated(g, k - 1)
                        if attn and 1 <= k <= NB:
                            rstd_x1(a, k - 1)
                        if attn and k == 0:
                            scale_x(a, 2)
                    else:
                        if attn and k < NB:
                            split_ctx(a, k)
                        if attn and k == 1:
                            scale_x(a, 3)
                        if more and k == NB:
                            scale_x(a + 1, 0)
                            scale_x(a + 1, 1)

            def weights_lo(k):
                pool.wait_ge(w_hi_ready, k + 2)
                if k < KD:
                    pool.tensor_tensor(wgu_lo[:, k, :], wgu_part(k), wgu_hi[:, k, :].bitcast(F32), ALU.subtract).then_inc(w_ready, 1)
                else:
                    pool.tensor_tensor(dn_lo[:], dn_raw[:], dn_hi[:].bitcast(F32), ALU.subtract).then_inc(w_ready, 1)

            def first():
                for b in range(NB):
                    scale_x(0, b)
                for k in range(NB + 2):
                    if k >= 2:
                        weights_lo(k - 2)
                    if 1 <= k <= NB:
                        rstd_x1(0, k - 1)
                    if k < NB:
                        split_ctx(0, k)
                scale_x(1, 0)
                scale_x(1, 1)
                weights_lo(KD)

            pool.memset(nhalf[:], -0.5).then_inc(set_up, 1)
            pool.wait_ge(set_up, 1)
            first()
            steps(pool, step)


def kernel(x, ctx_2048, mask_BxS2_bk0, L0_ffn_G, L0_ffn_gate_w, L0_ffn_up_w, L0_ffn_down_w, L0_ffn_lora_A, L0_ffn_lora_B):
    import concourse.bacc as bacc
    from concourse.bass_utils import run_bass_kernel_spmd

    def by_chunk(w):
        return w.reshape(KD, P, -1).transpose(1, 0, 2)

    def by_feature(v):
        return v.transpose(0, 2, 1).reshape(B, KD, P, S).transpose(0, 2, 1, 3)

    x, ctx = np.asarray(x), np.asarray(ctx_2048)
    mask = np.asarray(mask_BxS2_bk0).reshape(NG, NB, S)
    gate, up = (by_chunk(np.asarray(w).reshape(E * FE, D).T) for w in (L0_ffn_gate_w, L0_ffn_up_w))
    wgu = np.concatenate([gate, up], 2)
    ga = np.concatenate([by_chunk(np.asarray(L0_ffn_G)), by_chunk(np.asarray(L0_ffn_lora_A).reshape(LR, D).T)], 2)
    dn = np.concatenate([by_chunk(np.asarray(L0_ffn_down_w).transpose(0, 2, 1).reshape(E * FE, D)),
                         np.asarray(L0_ffn_lora_B).transpose(0, 2, 1).reshape(P, 1, D)], 1)
    sel = np.zeros((P, NC * P), np.float32)
    for e in range(E):
        sel[e, e * FE:(e + 1) * FE] = sel[E + e, e * FE:(e + 1) * FE] = 1
    earlier = np.tile(np.tril(np.ones((E, E), np.float32), -1).reshape(1, -1), (P, NB))
    consts = np.concatenate([np.eye(P, dtype=np.float32), sel, earlier], 1)

    arrays = {"x": x, "xT": by_feature(x), "ctx": ctx, "ctxT": by_feature(ctx), "mask": mask, "wgu": wgu, "ga": ga, "dn": dn, "consts": consts}
    arrays = {f"in_{n}": np.ascontiguousarray(a) for n, a in arrays.items()}
    nc = bacc.Bacc("TRN2", target_bir_lowering=False, num_devices=1)
    args = [nc.dram_tensor(n, a.shape, mybir.dt.from_np(a.dtype), kind="ExternalInput").ap() for n, a in arrays.items()]
    args.append(nc.dram_tensor("out_x", (B, S, D), F32, kind="ExternalOutput").ap())
    xattn_moe(nc, *args)
    return run_bass_kernel_spmd(nc, [arrays], core_ids=[0]).results[0]["out_x"]
```

```python
from contextlib import ExitStack

import numpy as np
import concourse.bass as bass
from concourse import mybir

F32 = mybir.dt.float32
F32R = mybir.dt.float32r
U8 = mybir.dt.uint8
ALU = mybir.AluOpType
ACT = mybir.ActivationFunctionType
AX = mybir.AxisListType

B, S, D = 64, 128, 512
P = 128
KD = D // P
E, FE, R = 8, 64, 16
NB = 4
NG = B // NB
T = NB * S
NC = E * FE // P
NU = 2 * NC + NB
LR = E * R
GA = E + LR
EPS = 1e-5
BIG = 1e30
RING = 3
H2_AT, READ_AT, ROUTE_AT, SCORES_AT = 1, 3, 3, 1
WEIGHTS0_AT, WEIGHTS_AT = 2, 0


def past(count, least):
    return not isinstance(count, int) or count >= least


def xattn_moe(nc, x, xT, ctx, ctxT, mask, wgu, ga, dn, consts, out):
    with ExitStack() as stack:
        def sb(name, shape, dt=F32):
            return stack.enter_context(nc.sbuf_tensor(name, [P] + shape, dt))

        def sem(name):
            return stack.enter_context(nc.semaphore(name))

        def bank(name):
            return stack.enter_context(nc.psum_tensor(name, [P, 512], F32))
        ffn_ps = [bank(f"ffn_ps{i}") for i in range(RING)]
        w_ps = bank("w_ps")
        mean_ps = bank("mean_ps")
        sr_ps = bank("sr_ps")
        pv_ps = bank("pv_ps")
        h2T_ps = bank("h2T_ps")

        wgu_hi, wgu_lo = sb("wgu_hi", [KD, 2 * E * FE], F32R), sb("wgu_lo", [KD, 2 * E * FE], F32R)
        ga_r = sb("ga_r", [KD, 2 * GA], F32R)
        dn_raw = sb("dn_raw", [NC + 1, D])
        dn_hi, dn_lo = sb("dn_hi", [NC + 1, D], F32R), sb("dn_lo", [NC + 1, D], F32R)
        const_sb = sb("const_sb", [P + NB * E * E])
        ident = const_sb[:, 0:P]
        earlier = const_sb[:, P:].rearrange("p (b e f) -> p b e f", b=NB, e=E)
        nhalf = sb("nhalf", [1])

        x_sb = sb("x_sb", [NB, D])
        xT_sb = sb("xT_sb", [NB, KD, P])
        ctx_sb = sb("ctx_sb", [NB, D])
        ctxT_sb = sb("ctxT_sb", [NB, KD, P])
        mask_sb = sb("mask_sb", [NB, S], U8)
        bias = sb("bias", [NB, S])
        valid, offset = sb("valid", [NB]), sb("offset", [NB])
        masked = sb("masked", [S])
        rowmax, negmax = sb("rowmax", [1]), sb("negmax", [1])
        prob, rowsum = sb("prob", [S]), sb("rowsum", [1])
        rinv, rinv_v = sb("rinv", [1]), sb("rinv_v", [1])
        pT_hi, pT_lo = sb("pT_hi", [S], F32R), sb("pT_lo", [S], F32R)
        ctx_hi, ctx_lo = sb("ctx_hi", [2, D], F32R), sb("ctx_lo", [2, D], F32R)
        x1 = sb("x1", [2, NB, D])
        h2 = sb("h2", [D])
        st1, mv1 = sb("st1", [6]), sb("mv1", [NB, 2])
        var1, scale1 = sb("var1", [NB]), sb("scale1", [NB])
        st2, mv2, ln2 = sb("st2", [6]), sb("mv2", [2]), sb("ln2", [3])

        h2T_hi, h2T_lo = sb("h2T_hi", [2, KD, T], F32R), sb("h2T_lo", [2, KD, T], F32R)
        router = sb("router", [NB, GA])
        ga_raw = router
        lmax, lexp, lsum, linv = sb("lmax", [NB]), sb("lexp", [NB, E]), sb("lsum", [NB]), sb("linv", [NB])
        gt, eq = sb("gt", [NB, E, E]), sb("eq", [NB, E, E])
        rank, rw = sb("rank", [NB, E]), sb("rw", [NB, E])
        half_w = sb("half_w", [E, NB])
        lrw = sb("lrw", [NB, LR])
        wT = sb("wT", [P])
        wb = sb("wb", [NC, T])
        work = sb("work", [4, T])
        th, t1, gw = work[:, 0, :], [work[:, 1, :], work[:, 3, :]], work[:, 2, :]
        gat_hi, gat_lo = sb("gat_hi", [NC + 1, T], F32R), sb("gat_lo", [NC + 1, T], F32R)

        w_dram = nc.dram_tensor("w_dram", [E * NB, P], F32).ap()
        w_by_expert = w_dram.rearrange("(e b) s -> e (b s)", e=E)

        wgu_loaded = [sem(f"wgu_loaded{k}") for k in range(KD)]
        ga_loaded, dn_loaded, ident_loaded, const_loaded = map(sem, ("ga_loaded", "dn_loaded", "ident_loaded", "const_loaded"))
        x_loaded = [sem(f"x_loaded{b}") for b in range(NB)]
        xT_loaded = [sem(f"xT_loaded{b}") for b in range(NB)]
        ctx_loaded = [sem(f"ctx_loaded{b}") for b in range(NB)]
        ctxT_loaded = [sem(f"ctxT_loaded{b}") for b in range(NB)]
        mask_loaded = sem("mask_loaded")
        stored = [sem(f"stored{b}") for b in range(NB)]
        w_hi_ready, w_ready = sem("w_hi_ready"), sem("w_ready")
        ga_ready, down_ready = sem("ga_ready"), sem("down_ready")
        set_up = sem("set_up")
        bias_ready, valid_ready = sem("bias_ready"), sem("valid_ready")
        st1_done, mv1_ready, scale1_step = map(sem, ("st1_done", "mv1_ready", "scale1_step"))
        st2_done, mv2_ready, ln2_step, h2_ready = map(sem, ("st2_done", "mv2_ready", "ln2_step", "h2_ready"))
        mean_done, centred = sem("mean_done"), sem("centred")
        scores_done, masked_ready, negmax_ready, prob_ready = map(sem, ("scores_done", "masked_ready", "negmax_ready", "prob_ready"))
        rinv_step, pT_done, pT_hi_ready, pT_lo_ready = map(sem, ("rinv_step", "pT_done", "pT_hi_ready", "pT_lo_ready"))
        ctx_hi_ready, ctx_lo_ready = sem("ctx_hi_ready"), sem("ctx_lo_ready")
        pv_done, x1_ready = sem("pv_done"), sem("x1_ready")
        h2T_done, h2T_hi_ready, h2T_lo_ready = map(sem, ("h2T_done", "h2T_hi_ready", "h2T_lo_ready"))
        router_done, lr_ready = sem("router_done"), sem("lr_ready")
        rt, lexp_ready, rw_ready = sem("rt"), sem("lexp_ready"), sem("rw_ready")
        wT_done, wT_ready = sem("wT_done"), sem("wT_ready")
        lrT_done, lr_hi_ready, lr_lo_ready = map(sem, ("lrT_done", "lr_hi_ready", "lr_lo_ready"))
        gate_up_done = sem("gate_up_done")
        th_ready, t1_ready, t2_ready, gw_ready, gat_hi_ready, gat_lo_ready = map(
            sem, ("th_ready", "t1_ready", "t2_ready", "gw_ready", "gat_hi_ready", "gat_lo_ready"))
        w_stored = sem("w_stored")
        wb_loaded = [sem(f"wb_loaded{c}") for c in range(NC)]
        down_done, out_ready = sem("down_done"), sem("out_ready")
        sp_waited, dve_waited, pool_waited = sem("sp_waited"), sem("dve_waited"), sem("pool_waited")
        RT = 11
        LEAD = 1

        def wgu_part(k):
            place = work[:] if k < KD // 2 else x1[:, 1, :, :]
            return place.rearrange("p c t -> p (c t)")[:, k % (KD // 2) * 2 * E * FE:(k % (KD // 2) + 1) * 2 * E * FE]

        block = stack.enter_context(nc.Block())

        def steps(engine, step):
            step(0, 0, True, True)
            with engine.Fori(0, (NG - 4) // 2) as i:
                step(2 * i + 1, 1, True, True)
                step(2 * i + 2, 0, True, True)
            step(NG - 3, 1, True, True)
            step(NG - 2, 0, True, False)
            step(NG - 1, 1, False, False)

        @block.sync
        def _(sp):
            def load_x(g, b):
                sp.dma_start(x_sb[:, b, :], x[NB * g + b]).then_inc(x_loaded[b], 16)

            def load_xT(g, b):
                sp.dma_start(xT_sb[:, b, :, :], xT[NB * g + b]).then_inc(xT_loaded[b], 16)

            def load_ctx(g, b):
                sp.dma_start(ctxT_sb[:, b, :, :], ctxT[NB * g + b]).then_inc(ctxT_loaded[b], 16)
                sp.dma_start(ctx_sb[:, b, :], ctx[NB * g + b]).then_inc(ctx_loaded[b], 16)

            def load_mask(g):
                sp.dma_start(mask_sb[:], mask[g].partition_broadcast(P)).then_inc(mask_loaded, 16)

            def spread_weights(g):
                sp.wait_ge(wT_ready, g + 1)
                if past(g, 1):
                    sp.wait_ge(gw_ready, NC * g)
                    sp.sem_inc(sp_waited, 1)
                sp.dma_start(w_dram, wT[0:E * NB, :]).then_inc(w_stored, 16)
                sp.wait_ge(w_stored, 16 * (g + 1))
                sp.sem_inc(sp_waited, 1)
                for e in range(E):
                    c, half = e * FE // P, e * FE % P
                    sp.dma_start(wb[half:half + FE, c, :], w_by_expert[e].partition_broadcast(FE)).then_inc(wb_loaded[c], 16)

            def load_weights(k):
                sp.dma_start(wgu_part(k), wgu[:, k, :]).then_inc(wgu_loaded[k], 16)

            load_x(0, 0)
            sp.dma_start(const_sb[:, 0:P], consts[:, 0:P]).then_inc(ident_loaded, 16)
            load_xT(0, 0)
            load_mask(0)
            load_ctx(0, 0)
            load_x(0, 1)
            load_xT(0, 1)
            load_ctx(0, 1)
            load_x(0, 2)
            load_xT(0, 2)
            sp.dma_start(ga_raw[:], ga).then_inc(ga_loaded, 16)
            load_x(0, 3)
            load_weights(0)
            load_ctx(0, 2)
            load_xT(0, 3)
            load_weights(1)
            load_ctx(0, 3)
            sp.dma_start(const_sb[:, P:], consts[:, P:]).then_inc(const_loaded, 16)
            load_weights(2)
            load_weights(3)
            sp.dma_start(dn_raw[:], dn).then_inc(dn_loaded, 16)

            def step(g, p, attn, more):
                a = g + 1
                if past(g, 0):
                    spread_weights(g)
                if more:
                    sp.wait_ge(bias_ready, a + 1)
                    sp.wait_ge(valid_ready, 2 * a + 2)
                    sp.sem_inc(sp_waited, 1)
                    load_mask(a + 1)
                    for b in range(NB):
                        n = NB * a + b
                        sp.wait_ge(x1_ready, n + 1)
                        sp.wait_ge(scores_done, n + 1)
                        sp.wait_ge(ctx_lo_ready, n + 1)
                        sp.sem_inc(sp_waited, 1)
                        load_x(a + 1, b)
                        load_xT(a + 1, b)
                        load_ctx(a + 1, b)
                if past(g, 0):
                    for b in range(NB):
                        sp.wait_ge(out_ready, NB * g + b + 1)
                        sp.sem_inc(sp_waited, 1)
                        sp.dma_start(out[NB * g + b], x1[:, p, b, :]).then_inc(stored[b], 16)

            step(-1, 1, True, True)
            steps(sp, step)
            for b in range(NB):
                sp.wait_ge(stored[b], 16 * NG)

        @block.tensor
        def _(pe):
            def three(psum, hi, lo, x_hi, x_lo, start, stop):
                pe.matmul(psum, hi, x_hi, start=start, stop=False)
                pe.matmul(psum, hi, x_lo, start=False, stop=False)
                return pe.matmul(psum, lo, x_hi, start=False, stop=stop)

            def turn_mean(a, b):
                n = NB * a + b
                pe.wait_ge(mv1_ready, n + 1)
                if past(n, 1):
                    pe.wait_ge(centred, n)
                pe.transpose(mean_ps[:, 0:P], mv1[:, b, 0:1].broadcast_to([P, P]), ident).then_inc(mean_done, 1)

            def scores(a, b):
                n = NB * a + b
                pe.wait_ge(centred, n + 1)
                pe.wait_ge(ctxT_loaded[b], 16 * (a + 1))
                if past(n, 1):
                    pe.wait_ge(masked_ready, n)
                if past(a, 1) and (b == 0 or b > LEAD):
                    pe.wait_ge(lr_ready, n if b == 0 else n - LEAD)
                for k in range(KD):
                    mm = pe.matmul(sr_ps[:, 0:S], xT_sb[:, b, k, :], ctxT_sb[:, b, k, :], start=(k == 0), stop=(k == KD - 1))
                mm.then_inc(scores_done, 1)

            def turn_prob(a, b):
                n = NB * a + b
                pe.wait_ge(prob_ready, n + 1)
                if past(n, 1):
                    pe.wait_ge(x1_ready, n)
                pe.transpose(pv_ps[:, 0:S], prob[:], ident).then_inc(pT_done, 1)

            def readout(a, b):
                n = NB * a + b
                pe.wait_ge(pT_lo_ready, n + 1)
                pe.wait_ge(ctx_lo_ready, n + 1)
                three(pv_ps[:], pT_hi[:], pT_lo[:], ctx_hi[:, b % 2, :], ctx_lo[:, b % 2, :], True, True).then_inc(pv_done, 1)

            def turn_h2(a, b):
                n = NB * a + b
                pe.wait_ge(h2_ready, n + 1)
                if past(n, 1):
                    pe.wait_ge(h2T_lo_ready, n)
                if b == 0 and past(a, 1):
                    pe.wait_ge(lr_lo_ready, a)
                for k in range(KD):
                    mm = pe.transpose(h2T_ps[:, k * P:(k + 1) * P], h2[:, k * P:(k + 1) * P], ident)
                mm.then_inc(h2T_done, 1)

            def route(a, q, b, ps=sr_ps):
                n = NB * a + b
                if b == 0 and not past(n, 1):
                    pe.wait_ge(ga_ready, 1)
                pe.wait_ge(h2T_lo_ready, n + 1)
                if past(a, 1):
                    pe.wait_ge(masked_ready, n + 1 + min(LEAD, NB - 1 - b))
                elif b:
                    pe.wait_ge(lr_ready, b)
                for k in range(KD):
                    pe.matmul(ps[:, 0:2 * GA], h2T_hi[:, q, k, b * S:(b + 1) * S], ga_r[:, k, :], start=(k == 0), stop=False)
                    mm = pe.matmul(ps[:, 0:2 * GA], h2T_lo[:, q, k, b * S:(b + 1) * S], ga_r[:, k, :], start=False, stop=(k == KD - 1))
                mm.then_inc(router_done, 1)

            def turn_weights(g):
                pe.wait_ge(rw_ready, g + 1)
                if past(g, 1):
                    pe.wait_ge(wT_ready, g)
                pe.transpose(w_ps[0:E * NB, 0:P], half_w[:].rearrange("p e b -> p (e b)"), ident).then_inc(wT_done, 1)
                pe.wait_ge(h2T_lo_ready, NB * g + NB)
                for b in range(NB):
                    mm = pe.transpose(h2T_ps[:, b * S:(b + 1) * S], lrw[:, b, :], ident)
                mm.then_inc(lrT_done, 1)

            def ffn_unit(g, p, u, between):
                ps = ffn_ps[u % RING]
                v = u - RING
                if v < 0:
                    if past(g, 1):
                        pe.wait_ge(out_ready, NB * g + v + 1)
                    elif u == 2:
                        pe.wait_ge(lr_ready, NB)
                elif v >= 2 * NC:
                    pe.wait_ge(out_ready, NB * g + v - 2 * NC + 1)
                elif v % 2 == 0:
                    pe.wait_ge(t1_ready, NC * g + v // 2 + 1)
                else:
                    pe.wait_ge(t2_ready, NC * g + v // 2 + 1)
                if u < 2 * NC:
                    c, col = u // 2, (u % 2) * E * FE + (u // 2) * P
                    if u == 0:
                        pe.wait_ge(h2T_lo_ready, NB * g + NB)
                        if not past(g, 1):
                            pe.wait_ge(w_ready, KD)
                    for k in range(KD):
                        between(k)
                        mm = three(ps[:], wgu_hi[:, k, col:col + P], wgu_lo[:, k, col:col + P],
                                   h2T_hi[:, p, k, :], h2T_lo[:, p, k, :], k == 0, k == KD - 1)
                    mm.then_inc(gate_up_done, 1)
                else:
                    b = u - 2 * NC
                    if b == 0:
                        if not past(g, 1):
                            pe.wait_ge(down_ready, 1)
                        pe.wait_ge(lr_lo_ready, g + 1)
                    order = [NC] + list(range(NC))
                    for j, c in enumerate(order):
                        between(j)
                        if b == 0 and c < NC:
                            pe.wait_ge(gat_lo_ready, NC * g + c + 1)
                        tok = slice(b * S, (b + 1) * S)
                        hi, lo, w_hi, w_lo = gat_hi[:, c, tok], gat_lo[:, c, tok], dn_hi[:, c, :], dn_lo[:, c, :]
                        mm = three(ps[:], hi, lo, w_hi, w_lo, j == 0, j == NC)
                    mm.then_inc(down_done, 1)

            def step(g, p, attn, more):
                a, q = g + 1, 1 - p
                for u in range(NU):
                    k, even = u // 2, u % 2 == 0
                    if attn and even and 1 <= k <= NB:
                        turn_prob(a, k - 1)

                    def between(done):
                        if attn and even and done == H2_AT and 2 <= k < NB + 2:
                            turn_h2(a, k - 2)
                        if attn and even and done == READ_AT and 1 <= k <= NB:
                            readout(a, k - 1)
                        if attn and even and done == ROUTE_AT + (k == NB + 1) and 2 <= k < NB + 2:
                            route(a, q, k - 2)
                        if attn and not even and done == SCORES_AT and k < NB:
                            scores(a, k)
                        if attn and not even and done == SCORES_AT and k < NB - 1:
                            turn_mean(a, k + 1)
                        if more and not even and done == SCORES_AT and k == NC + 1:
                            turn_mean(a + 1, 0)
                        if not even and k == 0 and done == (WEIGHTS_AT if past(g, 1) else WEIGHTS0_AT):
                            turn_weights(g)
                    ffn_unit(g, p, u, between)
                    if u < 2 * NC:
                        between(KD)

            def first():
                turn_mean(0, 0)
                for k in range(NB + 3):
                    if 1 <= k <= NB:
                        turn_prob(0, k - 1)
                    if k < NB:
                        scores(0, k)
                    if k < NB - 1:
                        turn_mean(0, k + 1)
                    if 1 <= k <= NB:
                        readout(0, k - 1)
                    if 2 <= k < NB + 2:
                        turn_h2(0, k - 2)
                    if k >= 3:
                        route(0, 0, k - 3, ffn_ps[2])
                    if k == NB + 1:
                        turn_mean(1, 0)

            pe.wait_ge(ident_loaded, 16)
            first()
            steps(pe, step)

        @block.scalar
        def _(act):
            def keep_h2T(a, g, q, b):
                n = NB * a + b
                act.wait_ge(h2T_done, n + 1)
                if b == 0 and past(g, 1):
                    act.wait_ge(gate_up_done, 2 * NC * g)
                act.copy(h2T_hi[:, q, :, b * S:(b + 1) * S], h2T_ps[:].rearrange("p (k s) -> p k s", k=KD)).then_inc(h2T_hi_ready, 1)

            def keep_pT(a, b):
                n = NB * a + b
                act.wait_ge(pT_done, n + 1)
                if past(n, 1):
                    act.wait_ge(pv_done, n)
                act.copy(pT_hi[:], pv_ps[:, 0:S]).then_inc(pT_hi_ready, 1)

            def split_gated(g, c):
                act.wait_ge(gw_ready, NC * g + c + 1)
                if c == 0 and past(g, 1):
                    act.wait_ge(down_done, NB * g)
                act.copy(gat_hi[:, c, :], gw).then_inc(gat_hi_ready, 1)

            def half_tanh(g, c):
                act.wait_ge(gate_up_done, 2 * NC * g + 2 * c + 1)
                if c or past(g, 1):
                    act.wait_ge(t1_ready, NC * g + c)
                act.activation(th, ffn_ps[2 * c % RING][:], ACT.Tanh, scale=0.5).then_inc(th_ready, 1)

            def keep_weights(g):
                act.wait_ge(wT_done, g + 1)
                if past(g, 1):
                    act.wait_ge(w_stored, 16 * g)
                act.copy(wT[0:E * NB, :], w_ps[0:E * NB, 0:P]).then_inc(wT_ready, 1)

            def keep_lrT(g):
                act.wait_ge(lrT_done, g + 1)
                if past(g, 1):
                    act.wait_ge(down_done, NB * g)
                act.copy(gat_hi[:, NC, :], h2T_ps[:]).then_inc(lr_hi_ready, 1)

            def softmax_exp(a, b):
                n = NB * a + b
                act.wait_ge(negmax_ready, n + 1)
                if past(n, 1):
                    act.wait_ge(pT_done, n)
                    act.wait_ge(rinv_step, 2 * n)
                act.activation(prob[:], masked[:], ACT.Exp, scale=scale1[:, b:b + 1], bias=negmax[:], accum_out=rowsum[:]).then_inc(prob_ready, 1)

            def split_ctx(a, b):
                n = NB * a + b
                act.wait_ge(ctx_loaded[b], 16 * (a + 1))
                if past(n, 2):
                    act.wait_ge(pv_done, n - 1)
                act.copy(ctx_hi[:, b % 2, :], ctx_sb[:, b, :]).then_inc(ctx_hi_ready, 1)

            def normalise_x1(a, b, p):
                n = NB * a + b
                act.wait_ge(ln2_step, 3 * n + 3)
                if past(n, 1):
                    act.wait_ge(h2T_done, n)
                act.activation(h2[:], x1[:, 1 - p, b, :], ACT.Identity, scale=ln2[:, 1:2], bias=ln2[:, 2:3]).then_inc(h2_ready, 1)

            def mask_bias(a):
                act.wait_ge(valid_ready, 2 * a + 2)
                if past(a, 1):
                    act.wait_ge(masked_ready, NB * a)
                for b in range(NB):
                    copy = act.activation(bias[:, b, :], mask_sb[:, b, :], ACT.Identity, scale=BIG, bias=offset[:, b:b + 1])
                copy.then_inc(bias_ready, 1)

            def router_exp(a):
                act.wait_ge(rt, RT * a + 2)
                act.activation(lexp[:], lexp[:], ACT.Exp).then_inc(lexp_ready, 1)

            def step(g, p, attn, more):
                a, q = g + 1, 1 - p
                for u in range(NU):
                    k, even = u // 2, u % 2 == 0
                    if even:
                        if attn and 1 <= k <= NB:
                            keep_pT(a, k - 1)
                        if attn and 2 <= k < NB + 2:
                            keep_h2T(a, g, q, k - 2)
                        if NC - 1 <= k <= NC:
                            split_gated(g, 2 * k - 5)
                        if k < NC:
                            half_tanh(g, k)
                        if attn and k == NB + 1:
                            router_exp(a)
                        if more and k == NB + 1:
                            mask_bias(a + 1)
                    else:
                        if k == 0:
                            keep_weights(g)
                        if attn and k < NB:
                            split_ctx(a, k)
                        if 2 <= k < NC:
                            split_gated(g, 2 * k - 4)
                        if attn and k < NB:
                            softmax_exp(a, k)
                        if k == 0:
                            keep_lrT(g)
                        if attn and 1 <= k <= NB:
                            normalise_x1(a, k - 1, p)

            def weights_hi(k):
                if k == 0:
                    act.wait_ge(ga_loaded, 16)
                    act.copy(ga_r[:, :, 0:GA], ga_raw[:]).then_inc(w_hi_ready, 1)
                elif k <= KD:
                    act.wait_ge(wgu_loaded[k - 1], 16)
                    act.copy(wgu_hi[:, k - 1, :], wgu_part(k - 1)).then_inc(w_hi_ready, 1)
                else:
                    act.wait_ge(dn_loaded, 16)
                    act.copy(dn_hi[:], dn_raw[:]).then_inc(w_hi_ready, 1)

            def first():
                mask_bias(0)
                split_ctx(0, 0)
                split_ctx(0, 1)
                for k in range(NB + 2):
                    if 1 <= k <= NB:
                        keep_pT(0, k - 1)
                        weights_hi(k)
                    if k >= 2:
                        normalise_x1(0, k - 2, 1)
                    if k < NB:
                        softmax_exp(0, k)
                    if k == 0:
                        weights_hi(k)
                    if k >= 2:
                        keep_h2T(0, -1, 0, k - 2)
                    if 1 <= k < NB - 1:
                        split_ctx(0, k + 1)
                mask_bias(1)
                weights_hi(NB + 1)
                router_exp(0)

            first()
            steps(act, step)

        @block.vector
        def _(dve):
            def stats_x(a, b):
                n = NB * a + b
                dve.wait_ge(x_loaded[b], 16 * (a + 1))
                if past(n, 1):
                    dve.wait_ge(mv1_ready, n)
                dve.bn_stats(st1[:], x_sb[:, b, :]).then_inc(st1_done, 1)
                dve.wait_ge(st1_done, n + 1)
                if past(a, 1):
                    dve.wait_ge(scale1_step, 2 * (n - NB) + 1)
                    dve.wait_ge(mean_done, n - NB + 1)
                dve.sem_inc(dve_waited, 1)
                dve.bn_aggr(mv1[:, b, :], st1[:]).then_inc(mv1_ready, 1)

            def centre(a, b):
                n = NB * a + b
                dve.wait_ge(mean_done, n + 1)
                dve.wait_ge(xT_loaded[b], 16 * (a + 1))
                dve.tensor_tensor(xT_sb[:, b, :, :], xT_sb[:, b, :, :],
                                  mean_ps[:, 0:P].rearrange("p (o s) -> p o s", o=1).broadcast_to([P, KD, P]),
                                  ALU.subtract).then_inc(centred, 1)

            def stats_x1(a, b, q):
                n = NB * a + b
                dve.wait_ge(x1_ready, n + 1)
                if past(n, 1):
                    dve.wait_ge(mv2_ready, n)
                dve.bn_stats(st2[:], x1[:, q, b, :]).then_inc(st2_done, 1)
                dve.wait_ge(st2_done, n + 1)
                if past(n, 1):
                    dve.wait_ge(ln2_step, 3 * n)
                dve.sem_inc(dve_waited, 1)
                dve.bn_aggr(mv2[:], st2[:]).then_inc(mv2_ready, 1)

            def any_valid(a):
                dve.wait_ge(mask_loaded, 16 * (a + 1))
                if past(a, 1):
                    dve.wait_ge(rinv_step, 2 * NB * a)
                    dve.wait_ge(bias_ready, a)
                dve.tensor_reduce(valid[:], mask_sb[:], AX.X, ALU.max).then_inc(valid_ready, 1)
                dve.wait_ge(valid_ready, 2 * a + 1)
                dve.tensor_scalar(offset[:], valid[:], -BIG, None, ALU.mult).then_inc(valid_ready, 1)

            def split_pT(a, b):
                n = NB * a + b
                dve.wait_ge(pT_hi_ready, n + 1)
                dve.tensor_tensor(pT_lo[:], pv_ps[:, 0:S], pT_hi[:].bitcast(F32), ALU.subtract).then_inc(pT_lo_ready, 1)

            def split_h2T(a, q, b):
                n = NB * a + b
                dve.wait_ge(h2T_hi_ready, n + 1)
                dve.tensor_tensor(h2T_lo[:, q, :, b * S:(b + 1) * S], h2T_ps[:].rearrange("p (k s) -> p k s", k=KD),
                                  h2T_hi[:, q, :, b * S:(b + 1) * S].bitcast(F32), ALU.subtract).then_inc(h2T_lo_ready, 1)

            def times_up(g, c):
                m = NC * g + c
                dve.wait_ge(gate_up_done, 2 * NC * g + 2 * c + 2)
                dve.wait_ge(t1_ready, m + 1)
                dve.tensor_tensor(t1[c % 2], t1[c % 2], ffn_ps[(2 * c + 1) % RING][:], ALU.mult).then_inc(t2_ready, 1)

            def times_weight(g, c):
                m = NC * g + c
                dve.wait_ge(wb_loaded[c], 32 * (g + 1))
                dve.wait_ge(t2_ready, m + 1)
                if c or past(g, 1):
                    dve.wait_ge(gat_lo_ready, m)
                dve.tensor_tensor(gw, t1[c % 2], wb[:, c, :], ALU.mult).then_inc(gw_ready, 1)

            def router_sums(a, b, ps=sr_ps):
                n = NB * a + b
                dve.wait_ge(router_done, n + 1)
                dve.tensor_reduce(router[:, b, :], ps[:, 0:2 * GA].rearrange("p (part f) -> p f part", part=2),
                                  AX.X, ALU.add).then_inc(lr_ready, 1)

            def twice_silu(g, c):
                dve.wait_ge(th_ready, NC * g + c + 1)
                if c == 1 and past(g, 1):
                    dve.wait_ge(gw_ready, NC * g)
                elif c == 0 and past(g, 1) or c >= 2:
                    dve.wait_ge(gw_ready, NC * g + c - 1)
                dve.scalar_tensor_tensor(out=t1[c % 2], in0=th, scalar=1.0, in1=ffn_ps[2 * c % RING][:],
                                         op0=ALU.add, op1=ALU.mult).then_inc(t1_ready, 1)

            def row_weights(a, b):
                n = NB * a + b
                dve.wait_ge(prob_ready, n + 1)
                if past(n, 1):
                    dve.wait_ge(x1_ready, n)
                dve.reciprocal(rinv[:], rowsum[:]).then_inc(rinv_step, 1)
                dve.wait_ge(rinv_step, 2 * n + 1)
                if b == 0:
                    dve.wait_ge(valid_ready, 2 * a + 2)
                dve.tensor_tensor(rinv_v[:], rinv[:], valid[:, b:b + 1], ALU.mult).then_inc(rinv_step, 1)

            def add_readout(a, q, b):
                n = NB * a + b
                dve.wait_ge(rinv_step, 2 * n + 2)
                dve.wait_ge(pv_done, n + 1)
                if b == 0 and q == 1 and not past(a, 2):
                    dve.wait_ge(w_ready, KD)
                if past(a, 2):
                    dve.wait_ge(stored[b], 16 * (a - 1))
                dve.scalar_tensor_tensor(out=x1[:, q, b, :], in0=pv_ps[:], scalar=rinv_v[:], in1=x_sb[:, b, :],
                                         op0=ALU.mult, op1=ALU.add).then_inc(x1_ready, 1)

            def mask_scores(a, b):
                n = NB * a + b
                dve.wait_ge(scores_done, n + 1)
                if b == 0:
                    dve.wait_ge(bias_ready, a + 1)
                if past(n, 1):
                    dve.wait_ge(prob_ready, n)
                dve.sem_inc(dve_waited, 1)
                dve.tensor_tensor_reduce(masked[:], sr_ps[:, 0:S], bias[:, b, :], 1.0, -3e38, ALU.add, ALU.max,
                                         rowmax[:]).then_inc(masked_ready, 1)
                dve.wait_ge(masked_ready, n + 1)
                dve.wait_ge(scale1_step, 2 * n + 2)
                dve.tensor_scalar(negmax[:], rowmax[:], scale1[:, b:b + 1], -1.0, ALU.mult, ALU.mult).then_inc(negmax_ready, 1)

            def add_ffn(g, p, b):
                dve.wait_ge(down_done, NB * g + b + 1)
                dve.tensor_tensor(x1[:, p, b, :], ffn_ps[(2 * NC + b) % RING][:], x1[:, p, b, :], ALU.add).then_inc(out_ready, 1)

            def split_lr(g):
                dve.wait_ge(lr_hi_ready, g + 1)
                dve.tensor_tensor(gat_lo[:, NC, :], h2T_ps[:], gat_hi[:, NC, :].bitcast(F32), ALU.subtract).then_inc(lr_lo_ready, 1)

            def route(a):
                def over(v):
                    return v.rearrange("p (b o) -> p b o", o=1).broadcast_to([P, NB, E])
                s = RT * a
                logits, lr = router[:, :, 0:E], router[:, :, E:]
                dve.wait_ge(lr_ready, NB * a + NB)
                dve.tensor_reduce(lmax[:], logits, AX.X, ALU.max).then_inc(rt, 1)
                dve.wait_ge(rt, s + 1)
                dve.tensor_tensor(lexp[:], logits, over(lmax[:]), ALU.subtract).then_inc(rt, 1)
                dve.wait_ge(lexp_ready, a + 1)
                dve.tensor_reduce(lsum[:], lexp[:], AX.X, ALU.add).then_inc(rt, 1)
                dve.wait_ge(rt, s + 3)
                dve.reciprocal(linv[:], lsum[:]).then_inc(rt, 1)
                dve.wait_ge(rt, s + 4)
                dve.tensor_tensor(lexp[:], lexp[:], over(linv[:]), ALU.mult).then_inc(rt, 1)
                dve.wait_ge(rt, s + 5)
                own = lexp[:].rearrange("p b (e o) -> p b e o", o=1).broadcast_to([P, NB, E, E])
                other = lexp[:].rearrange("p b (o e) -> p b o e", o=1).broadcast_to([P, NB, E, E])
                dve.tensor_tensor(gt[:], other, own, ALU.is_gt).then_inc(rt, 1)
                dve.tensor_tensor(eq[:], other, own, ALU.is_equal).then_inc(rt, 1)
                dve.wait_ge(rt, s + 7)
                dve.tensor_tensor(eq[:], eq[:], earlier, ALU.mult).then_inc(rt, 1)
                dve.wait_ge(rt, s + 8)
                dve.tensor_tensor(gt[:], gt[:], eq[:], ALU.add).then_inc(rt, 1)
                dve.wait_ge(rt, s + 9)
                dve.tensor_reduce(rank[:], gt[:], AX.X, ALU.add).then_inc(rt, 1)
                dve.wait_ge(rt, s + 10)
                dve.scalar_tensor_tensor(out=rw[:], in0=rank[:], scalar=1.5, in1=lexp[:], op0=ALU.is_lt, op1=ALU.mult).then_inc(rt, 1)
                dve.wait_ge(rt, s + 11)
                if past(a, 1):
                    dve.wait_ge(lrT_done, a)
                dve.tensor_scalar(half_w[:].rearrange("p e b -> p b e"), rw[:], 0.5, None, ALU.mult)
                dve.tensor_tensor(lrw[:].rearrange("p b (e r) -> p b e r", e=E), lr.rearrange("p b (e r) -> p b e r", e=E),
                                  rw[:].rearrange("p b (e o) -> p b e o", o=1).broadcast_to([P, NB, E, R]),
                                  ALU.mult).then_inc(rw_ready, 1)

            def step(g, p, attn, more):
                a, q = g + 1, 1 - p
                for u in range(NU):
                    k, even = u // 2, u % 2 == 0
                    if even:
                        if 1 <= k <= NC:
                            times_up(g, k - 1)
                        if attn and 1 <= k <= NB:
                            split_pT(a, k - 1)
                        if k == NC:
                            times_weight(g, NC - 1)
                        if attn and 1 <= k <= NB:
                            row_weights(a, k - 1)
                        if attn and k == 1:
                            stats_x(a, NB - 1)
                        if attn and 2 <= k < NB + 2:
                            split_h2T(a, q, k - 2)
                        if k == NC + 1:
                            add_ffn(g, p, 1)
                        if attn and 1 <= k <= NB:
                            add_readout(a, q, k - 1)
                        if attn and 2 <= k < NB + 2:
                            router_sums(a, k - 2)
                        if attn and 1 <= k <= NB:
                            stats_x1(a, k - 1, q)
                        if 2 <= k < NC:
                            times_weight(g, 2 * k - 4)
                        if more and k == NB:
                            stats_x(a + 1, 0)
                    else:
                        if attn and k < NB:
                            mask_scores(a, k)
                        if k < NC:
                            twice_silu(g, k)
                        if attn and k < NB - 1:
                            centre(a, k + 1)
                        if k == 2:
                            times_weight(g, 1)
                        if k == 0:
                            split_lr(g)
                        if k == NC:
                            add_ffn(g, p, 0)
                        if more and k == NB:
                            any_valid(a + 1)
                        if more and k == NB:
                            for b in range(1, NB - 1):
                                stats_x(a + 1, b)
                        if k == NC + 1:
                            add_ffn(g, p, 2)
                        if attn and k == NB + 1:
                            route(a)
                        if more and k == NB + 1:
                            centre(a + 1, 0)
                        if k == NC + 1:
                            add_ffn(g, p, 3)

            def first():
                stats_x(0, 0)
                any_valid(0)
                centre(0, 0)
                stats_x(0, 1)
                for k in range(NB + 3):
                    if 1 <= k <= NB:
                        split_pT(0, k - 1)
                    if k < NB:
                        mask_scores(0, k)
                    if 1 <= k <= NB:
                        row_weights(0, k - 1)
                    if k < NB - 1:
                        centre(0, k + 1)
                    if k < 2:
                        stats_x(0, k + 2)
                    if k == NB:
                        any_valid(1)
                    if 1 <= k <= NB:
                        add_readout(0, 0, k - 1)
                        stats_x1(0, k - 1, 0)
                    if 2 <= k < NB + 2:
                        split_h2T(0, 0, k - 2)
                    if k == NB:
                        dve.wait_ge(w_hi_ready, KD + 1)
                        dve.tensor_tensor(wgu_lo[:, KD - 1, :], wgu_part(KD - 1), wgu_hi[:, KD - 1, :].bitcast(F32),
                                          ALU.subtract).then_inc(w_ready, 1)
                    if k == 1:
                        dve.wait_ge(w_hi_ready, 1)
                        dve.tensor_tensor(ga_r[:, :, GA:], ga_raw[:], ga_r[:, :, 0:GA].bitcast(F32), ALU.subtract).then_inc(ga_ready, 1)
                    if k >= 3:
                        router_sums(0, k - 3, ffn_ps[2])
                    if k == NB:
                        stats_x(1, 0)
                    if k == NB + 1:
                        centre(1, 0)
                        stats_x(1, 1)
                dve.wait_ge(const_loaded, 16)
                route(0)
                stats_x(1, 2)

            first()
            steps(dve, step)

        @block.gpsimd
        def _(pool):
            def scale_x(a, b):
                n = NB * a + b
                pool.wait_ge(mv1_ready, n + 1)
                if past(a, 1):
                    pool.wait_ge(prob_ready, n - NB + 1)
                pool.sem_inc(pool_waited, 1)
                pool.tensor_scalar(var1[:, b:b + 1], mv1[:, b, 1:2], float(D), EPS * D, ALU.mult, ALU.add).then_inc(scale1_step, 1)
                pool.wait_ge(scale1_step, 2 * n + 1)
                pool.tensor_tensor(scale1[:, b:b + 1], var1[:, b:b + 1], nhalf[:], ALU.pow).then_inc(scale1_step, 1)

            def rstd_x1(a, b):
                n = NB * a + b
                pool.wait_ge(mv2_ready, n + 1)
                if past(n, 1):
                    pool.wait_ge(h2_ready, n)
                pool.sem_inc(pool_waited, 1)
                pool.tensor_scalar(ln2[:, 0:1], mv2[:, 1:2], EPS, None, ALU.add).then_inc(ln2_step, 1)
                pool.wait_ge(ln2_step, 3 * n + 1)
                pool.tensor_tensor(ln2[:, 1:2], ln2[:, 0:1], nhalf[:], ALU.pow).then_inc(ln2_step, 1)
                pool.wait_ge(ln2_step, 3 * n + 2)
                pool.sem_inc(pool_waited, 1)
                pool.tensor_scalar(ln2[:, 2:3], mv2[:, 0:1], ln2[:, 1:2], -1.0, ALU.mult, ALU.mult).then_inc(ln2_step, 1)

            def split_ctx(a, b):
                n = NB * a + b
                pool.wait_ge(ctx_hi_ready, n + 1)
                pool.tensor_tensor(ctx_lo[:, b % 2, :], ctx_sb[:, b, :], ctx_hi[:, b % 2, :].bitcast(F32), ALU.subtract).then_inc(ctx_lo_ready, 1)

            def split_gated(g, c):
                pool.wait_ge(gat_hi_ready, NC * g + c + 1)
                pool.tensor_tensor(gat_lo[:, c, :], gw, gat_hi[:, c, :].bitcast(F32), ALU.subtract).then_inc(gat_lo_ready, 1)

            def step(g, p, attn, more):
                a = g + 1
                for u in range(NU):
                    k, even = u // 2, u % 2 == 0
                    if even:
                        if NC - 1 <= k <= NC:
                            split_gated(g, 2 * k - 5)
                        if attn and 1 <= k <= NB:
                            rstd_x1(a, k - 1)
                        if attn and k == 1:
                            scale_x(a, NB - 1)
                    else:
                        if 2 <= k < NC:
                            split_gated(g, 2 * k - 4)
                        if attn and k < NB:
                            split_ctx(a, k)
                        if more and k == NB:
                            for b in range(NB - 1):
                                scale_x(a + 1, b)

            def gate_up_lo(k):
                pool.wait_ge(w_hi_ready, k + 2)
                pool.tensor_tensor(wgu_lo[:, k, :], wgu_part(k), wgu_hi[:, k, :].bitcast(F32), ALU.subtract).then_inc(w_ready, 1)

            def down_lo():
                pool.wait_ge(w_hi_ready, KD + 2)
                pool.tensor_tensor(dn_lo[:], dn_raw[:], dn_hi[:].bitcast(F32), ALU.subtract).then_inc(down_ready, 1)

            def first():
                scale_x(0, 0)
                scale_x(0, 1)
                split_ctx(0, 0)
                scale_x(0, 2)
                split_ctx(0, 1)
                scale_x(0, 3)
                for k in range(1, NB + 1):
                    rstd_x1(0, k - 1)
                    if k < NB - 1:
                        split_ctx(0, k + 1)
                    if k < NB:
                        gate_up_lo(k - 1)
                scale_x(1, 0)
                scale_x(1, 1)
                down_lo()
                scale_x(1, 2)

            pool.memset(nhalf[:], -0.5).then_inc(set_up, 1)
            pool.wait_ge(set_up, 1)
            first()
            steps(pool, step)


def kernel(x, ctx_2048, mask_BxS2_bk0, L0_ffn_G, L0_ffn_gate_w, L0_ffn_up_w, L0_ffn_down_w, L0_ffn_lora_A, L0_ffn_lora_B):
    import concourse.bacc as bacc
    from concourse.bass_utils import run_bass_kernel_spmd

    def by_chunk(w):
        return w.reshape(KD, P, -1).transpose(1, 0, 2)

    def by_feature(v):
        return v.transpose(0, 2, 1).reshape(B, KD, P, S).transpose(0, 2, 1, 3)

    x, ctx = np.asarray(x), np.asarray(ctx_2048)
    mask = np.asarray(mask_BxS2_bk0).reshape(NG, NB, S)
    gate, up = (by_chunk(np.asarray(w).reshape(E * FE, D).T) for w in (L0_ffn_gate_w, L0_ffn_up_w))
    wgu = np.concatenate([gate, up], 2)
    ga = np.concatenate([by_chunk(np.asarray(L0_ffn_G)), by_chunk(np.asarray(L0_ffn_lora_A).reshape(LR, D).T)], 2)
    dn = np.concatenate([by_chunk(np.asarray(L0_ffn_down_w).transpose(0, 2, 1).reshape(E * FE, D)),
                         np.asarray(L0_ffn_lora_B).transpose(0, 2, 1).reshape(P, 1, D)], 1)
    earlier = np.tile(np.tril(np.ones((E, E), np.float32), -1).reshape(1, -1), (P, NB))
    consts = np.concatenate([np.eye(P, dtype=np.float32), earlier], 1)

    arrays = {"x": x, "xT": by_feature(x), "ctx": ctx, "ctxT": by_feature(ctx), "mask": mask, "wgu": wgu, "ga": ga, "dn": dn, "consts": consts}
    arrays = {f"in_{n}": np.ascontiguousarray(a) for n, a in arrays.items()}
    nc = bacc.Bacc("TRN2", target_bir_lowering=False, num_devices=1)
    args = [nc.dram_tensor(n, a.shape, mybir.dt.from_np(a.dtype), kind="ExternalInput").ap() for n, a in arrays.items()]
    args.append(nc.dram_tensor("out_x", (B, S, D), F32, kind="ExternalOutput").ap())
    xattn_moe(nc, *args)
    return run_bass_kernel_spmd(nc, [arrays], core_ids=[0]).results[0]["out_x"]
```
